# Optimizing a Trainium2 kernel written in Bass

```python
import numpy as np
import jax
import jax.numpy as jnp

def _softmax(x, axis=-1):
    return jax.nn.softmax(x, axis=axis)

def _gelu(x):
    return jax.nn.gelu(x, approximate=True)

def _silu(x):
    return jax.nn.silu(x)

def _sigmoid(x):
    return jax.nn.sigmoid(x)

def _layernorm(x, axis=-1, eps=1e-05):
    m = jnp.mean(x, axis=axis, keepdims=True)
    v = jnp.var(x, axis=axis, keepdims=True)
    return (x - m) / jnp.sqrt(v + eps)

def _scatter_add(tgt, idx, src, axis=0):
    return tgt.at[idx].add(src)

def _segment_sum(src, seg, n):
    return jax.ops.segment_sum(src, seg, n)
kernel_name = 'mk_adj_resnorm_d4_adj_r2_cd297c'

def setup_inputs(seed: int=0):
    np.random.seed(seed)
    _w = jnp.asarray

    def _rec_inputs():
        import jax
        import jax.numpy as jnp
        _gk = jax.random.key(seed)
        x = -0.000929 + 1 * jax.random.normal(jax.random.fold_in(_gk, 1), (8, 2048, 64), jnp.float32)
        _w = (1.0 + jnp.arange(2048, dtype=jnp.float32)) ** (-0.5)
        _w = _w / _w.mean()
        _pij = jnp.clip(0.0078125 * _w[:, None] * _w[None, :], 0.0, 1.0)
        _a = jax.random.uniform(jax.random.fold_in(_gk, 2), (8, 2048, 2048)) < _pij
        _a = jnp.logical_or(_a, jnp.eye(2048, dtype=bool))
        _af = _a.astype(jnp.float32)
        _af = _af * jax.random.uniform(jax.random.fold_in(_gk, 3), (8, 2048, 2048), jnp.float32, 0.05, 1)
        adj = _af
        _nm = jnp.ones((8, 2048), dtype=bool)
        nodemask = jnp.where(_nm, 1.0, 0.0).astype(jnp.float32)
        return (x, adj, nodemask)
    x, adj, nodemask = _rec_inputs()

    def _L0_gnn_setup():
        import jax, jax.numpy as jnp
        import numpy as np
        B, N, C, R = (4, 2048, 64, 16)
        EPS = 1e-12
        key = jax.random.key(seed)
        k_x, k_w, k_u = jax.random.split(key, 3)
        x = jax.random.normal(k_x, (B, N, C), dtype=jnp.float32)
        W = jax.random.uniform(k_w, (B, N, N), dtype=jnp.float32)
        U = 0.01 * jax.random.normal(k_u, (N, R), dtype=jnp.float32)
        w_scale = jnp.asarray(1.0, dtype=jnp.float32)
        return {'x': x, 'W': W, 'U': U, 'w_scale': w_scale}
    _L0_gnn_all = _L0_gnn_setup()
    _L0_gnn_in = {k: v for k, v in _L0_gnn_all.items() if k in ('U', 'w_scale')}
    del _L0_gnn_all

    def _L1_gnn_setup():
        import jax, jax.numpy as jnp
        import numpy as np
        NORM = 1.0

        def _glorot(key, shape):
            fan_in, fan_out = shape
            lim = float(np.sqrt(6.0 / (fan_in + fan_out)))
            return jax.random.uniform(key, shape, jnp.float32, -lim, lim)

        def _gcn_layer(h, adj, W, b):
            msg = h @ W + b
            agg = jnp.einsum('bij,bjd->bid', adj, msg) / NORM
            return jax.nn.relu(agg)
        key = jax.random.key(seed)
        ks = jax.random.split(key, 12)
        B, N = (8, 1024)
        latent, hidden, out_dim = (64, 128, 64)
        inp = {'latent_features': jax.random.normal(ks[0], (B, N, latent), jnp.float32), 'adjacency_matrix': jax.random.uniform(ks[1], (B, N, N), jnp.float32), 'node_mask': jnp.ones((B, N, 1), jnp.float32), 'W0': _glorot(ks[2], (latent, hidden)), 'b0': jnp.zeros((hidden,), jnp.float32), 'W1': _glorot(ks[3], (hidden, hidden)), 'b1': jnp.zeros((hidden,), jnp.float32), 'W2': _glorot(ks[4], (hidden, hidden)), 'b2': jnp.zeros((hidden,), jnp.float32), 'Wout': _glorot(ks[5], (hidden, out_dim)), 'bout': jnp.zeros((out_dim,), jnp.float32)}
        return inp
    _L1_gnn_all = _L1_gnn_setup()
    _L1_gnn_in = {k: v for k, v in _L1_gnn_all.items() if k in ('W0', 'b0', 'W1', 'b1', 'W2', 'b2', 'Wout', 'bout')}
    del _L1_gnn_all

    def _L2_gnn_setup():
        import jax, jax.numpy as jnp
        import numpy as np
        from math import sqrt
        B, N, C_IN, C_OUT = (4, 2048, 64, 64)
        key = jax.random.key(seed)
        k1, k2, k3, k4 = jax.random.split(key, 4)
        X = jax.random.normal(k1, (B, N, C_IN), dtype=jnp.float32)
        A = jax.random.uniform(k2, (B, N, N), dtype=jnp.float32)
        std = sqrt(2.0 / C_IN)
        W_neighbors = jax.random.normal(k3, (C_IN, C_OUT), dtype=jnp.float32) * std
        W_self = jax.random.normal(k4, (C_IN, C_OUT), dtype=jnp.float32) * std
        bias = jnp.zeros((1, C_OUT), dtype=jnp.float32)
        return {'X': X, 'A': A, 'W_neighbors': W_neighbors, 'W_self': W_self, 'bias': bias}
    _L2_gnn_all = _L2_gnn_setup()
    _L2_gnn_in = {k: v for k, v in _L2_gnn_all.items() if k in ('W_neighbors', 'W_self', 'bias')}
    del _L2_gnn_all

    def _L3_gnn_setup():
        import jax, jax.numpy as jnp
        import numpy as np
        B, N, F, U = (16, 1024, 64, 64)
        key = jax.random.key(seed)
        k1, k2, k3 = jax.random.split(key, 3)
        node_features = jax.random.normal(k1, (B, N, F), dtype=jnp.float32)
        adjacency_matrix = (jax.random.uniform(k2, (B, N, N)) < 0.01).astype(jnp.float32)
        kernel = jax.random.normal(k3, (F, U), dtype=jnp.float32) * (1.0 / np.sqrt(F))
        return {'node_features': node_features, 'adjacency_matrix': adjacency_matrix, 'kernel': kernel}
    _L3_gnn_all = _L3_gnn_setup()
    _L3_gnn_in = {k: v for k, v in _L3_gnn_all.items() if k in ('kernel',)}
    del _L3_gnn_all
    return {'x': x, 'adj': adj, 'nodemask': nodemask, 'L0_gnn_U': _L0_gnn_in['U'], 'L0_gnn_w_scale': _L0_gnn_in['w_scale'], 'L1_gnn_W0': _L1_gnn_in['W0'], 'L1_gnn_b0': _L1_gnn_in['b0'], 'L1_gnn_W1': _L1_gnn_in['W1'], 'L1_gnn_b1': _L1_gnn_in['b1'], 'L1_gnn_W2': _L1_gnn_in['W2'], 'L1_gnn_b2': _L1_gnn_in['b2'], 'L1_gnn_Wout': _L1_gnn_in['Wout'], 'L1_gnn_bout': _L1_gnn_in['bout'], 'L2_gnn_W_neighbors': _L2_gnn_in['W_neighbors'], 'L2_gnn_W_self': _L2_gnn_in['W_self'], 'L2_gnn_bias': _L2_gnn_in['bias'], 'L3_gnn_kernel': _L3_gnn_in['kernel']}

def reference(x, adj, nodemask, L0_gnn_U, L0_gnn_w_scale, L1_gnn_W0, L1_gnn_b0, L1_gnn_W1, L1_gnn_b1, L1_gnn_W2, L1_gnn_b2, L1_gnn_Wout, L1_gnn_bout, L2_gnn_W_neighbors, L2_gnn_W_self, L2_gnn_bias, L3_gnn_kernel):
    import jax
    import jax.numpy as jnp

    def _L0_gnn_ref(x, W, U, w_scale):
        import jax, jax.numpy as jnp
        import numpy as np
        B, N, C, R = (4, 2048, 64, 16)
        EPS = 1e-12
        Ws = 0.5 * (W + jnp.swapaxes(W, -1, -2))
        A = jax.nn.sigmoid(U @ U.T)
        K = Ws * A[None, :, :]
        deg = jnp.maximum(K.sum(axis=-1), EPS)
        d = jax.lax.rsqrt(deg)
        K = K * d[:, :, None] * d[:, None, :]
        return w_scale * jnp.einsum('bnm,bmc->bnc', K, x)

    def _L1_gnn_ref(latent_features, adjacency_matrix, node_mask, W0, b0, W1, b1, W2, b2, Wout, bout):
        import jax, jax.numpy as jnp
        import numpy as np
        NORM = 1.0

        def _glorot(key, shape):
            fan_in, fan_out = shape
            lim = float(np.sqrt(6.0 / (fan_in + fan_out)))
            return jax.random.uniform(key, shape, jnp.float32, -lim, lim)

        def _gcn_layer(h, adj, W, b):
            msg = h @ W + b
            agg = jnp.einsum('bij,bjd->bid', adj, msg) / NORM
            return jax.nn.relu(agg)
        h = _gcn_layer(latent_features, adjacency_matrix, W0, b0)
        h = _gcn_layer(h, adjacency_matrix, W1, b1)
        h = _gcn_layer(h, adjacency_matrix, W2, b2)
        return (h @ Wout + bout) * node_mask

    def _L2_gnn_ref(X, A, W_neighbors, W_self, bias):
        import jax, jax.numpy as jnp
        import numpy as np
        from math import sqrt
        B, N, C_IN, C_OUT = (4, 2048, 64, 64)
        deg = jnp.sum(A, axis=1)[..., None]
        inv_deg = jnp.where(deg != 0, 1.0 / deg, 0.0)
        message = jnp.einsum('bij,bjc->bic', A, X) * inv_deg
        out = message @ W_neighbors + X @ W_self + bias
        return out

    def _L3_gnn_ref(node_features, adjacency_matrix, kernel):
        import jax, jax.numpy as jnp
        import numpy as np
        B, N, F, U = (16, 1024, 64, 64)
        n = adjacency_matrix.shape[-1]
        adj = adjacency_matrix + jnp.eye(n, dtype=adjacency_matrix.dtype)
        row_sum = jnp.sum(adj, axis=-1)
        d_inv_sqrt = jnp.where(row_sum > 0, row_sum ** (-0.5), 0.0)
        norm_adj = d_inv_sqrt[:, :, None] * adj * d_inv_sqrt[:, None, :]
        transformed = jnp.einsum('bnf,fu->bnu', node_features, kernel)
        out = jnp.einsum('bnm,bmu->bnu', norm_adj, transformed)
        return jax.nn.relu(out)
    x = _layernorm(x + _L0_gnn_ref(x, adj, L0_gnn_U, L0_gnn_w_scale), axis=-1)
    x = _layernorm(x + _L1_gnn_ref(x, adj, nodemask[..., None], L1_gnn_W0, L1_gnn_b0, L1_gnn_W1, L1_gnn_b1, L1_gnn_W2, L1_gnn_b2, L1_gnn_Wout, L1_gnn_bout), axis=-1)
    x = _layernorm(x + _L2_gnn_ref(x, adj, L2_gnn_W_neighbors, L2_gnn_W_self, L2_gnn_bias), axis=-1)
    x = _layernorm(x + _L3_gnn_ref(x, adj, L3_gnn_kernel), axis=-1)
    return x

_drawn_inputs = setup_inputs


def setup_inputs(seed=0):
    import zlib

    import numpy as np

    out = dict(_drawn_inputs(seed))
    spreads = {'L1_gnn_b0': (0.0, 0.1),
     'L1_gnn_b1': (0.0, 0.1),
     'L1_gnn_b2': (0.0, 0.8),
     'L1_gnn_bout': (0.0, 2.0),
     'L2_gnn_bias': (0.0, 0.1)}
    factors = {'L0_gnn_U': 64.0}
    for name, (base, spread) in spreads.items():
        noise = np.random.default_rng([zlib.crc32(name.encode()), seed]).standard_normal(out[name].shape)
        drawn = base * np.exp(spread * noise) if base else spread * noise
        out[name] = jnp.asarray(drawn.astype(out[name].dtype))
    for name, factor in factors.items():
        out[name] = (out[name] * factor).astype(out[name].dtype)
    return out
```

```python
from contextlib import ExitStack

import numpy as np

import concourse.bass as bass
from concourse import mybir


def adjacency_stack_kernel(
    nc: bass.Bass,
    x: bass.AP,
    adj: bass.AP,
    nodemask: bass.AP,
    U: bass.AP,
    w_scale: bass.AP,
    W0: bass.AP,
    b0: bass.AP,
    W1: bass.AP,
    b1: bass.AP,
    W2: bass.AP,
    b2: bass.AP,
    Wout: bass.AP,
    bout: bass.AP,
    W_neighbors: bass.AP,
    W_self: bass.AP,
    bias: bass.AP,
    W_l3: bass.AP,
    out: bass.AP,
):
    fp32 = mybir.dt.float32
    bf16 = mybir.dt.bfloat16
    ALU = mybir.AluOpType
    ACT = mybir.ActivationFunctionType
    X = mybir.AxisListType.X

    B, N, C = x.shape
    HID = W1.shape[0]
    R = U.shape[1]
    P = 128
    T = N // P
    G = 4
    NG = T // G
    GN = G * P
    SLOTS = 4
    T_LOADS = T // SLOTS
    K_LOADS = (T - SLOTS) // SLOTS
    LOADS = T_LOADS + K_LOADS
    DMA = 16
    POOL_COLS = 1152
    DEG_EPS = 1e-12
    LN_EPS = 1e-5
    HALF = N // 2
    assert P == 2 * C and HID == P and T == 16 and NG == 4

    with ExitStack() as ctx:
        def sb(name, shape, dt=fp32):
            return ctx.enter_context(nc.sbuf_tensor(name, shape, dt))

        def sem(name):
            return ctx.enter_context(nc.semaphore(name))

        adjT = sb("adjT", [P, T, N])
        rows = sb("rows", [P, SLOTS, N])
        work = sb("work", [P, 3, N])
        ustat = sb("ustat", [P, N], bf16)
        umov = sb("umov", [P, N], bf16)
        xa = sb("xa", [P, T, C])
        xb = sb("xb", [P, T, C])
        w0s = sb("w0s", [P, HID])
        w1 = sb("w1", [P, HID])
        w2 = sb("w2", [P, HID])
        wout = sb("wout", [P, C])
        wns = sb("wns", [P, C])
        wss = sb("wss", [P, P])
        wks = sb("wks", [P, C])
        ident = sb("ident", [P, P])
        b0b = sb("b0b", [P, HID])
        b1b = sb("b1b", [P, HID])
        b2b = sb("b2b", [P, HID])
        boutb = sb("boutb", [P, C])
        biasb = sb("biasb", [P, C])
        wsc = sb("wsc", [P, 1])
        mask = sb("mask", [P, B, T])
        neghalf = sb("neghalf", [P, T])
        rowsum = sb("rowsum", [P, T])
        colsum = sb("colsum", [P, T])
        kpart = sb("kpart", [P, T, 2])
        deg = sb("deg", [P, T])
        dl0 = sb("dl0", [P, T])
        dw = sb("dw", [P, T])
        invdeg = sb("invdeg", [P, T])
        dinv = sb("dinv", [P, T])
        tiny = sb("tiny", [P, 3, T])
        total = sb("total", [P, G])
        var = sb("var", [P, G])
        rstd = sb("rstd", [P, G])
        xs = sb("xs", [P, 2, C])

        hT = work[:, 0, :]
        ys = work[:, 0, 0:T * C].rearrange("p (t c) -> p t c", c=C)
        msg = work[:, 1, :].rearrange("p (t d) -> p t d", d=HID)
        xT = work[:, 1, 0:T * C].rearrange("p (u n) -> p u n", n=P)
        agg = work[:, 2, 0:2 * GN].rearrange("p (s n) -> p s n", n=GN)
        yv = work[:, 2, 1024:1280].rearrange("p (t c) -> p t c", c=C)
        sq = work[:, 2, 1280:1536].rearrange("p (t c) -> p t c", c=C)
        diag = xb[:, :, :].rearrange("p (s t) c -> p s (t c)", s=2)
        adjT_flat = adjT[:, :, :].rearrange("p j i -> p (j i)")

        u_nat = adjT[:, 0, 0:T * R].rearrange("p (t r) -> p t r", r=R)
        u_rest = adjT[:, 1, 0:T * R].rearrange("p (t r) -> p t r", r=R)
        ustat_nat = adjT[:, 2, 0:HALF].bitcast(bf16).rearrange("p (t s r) -> p t s r", s=8, r=R)
        umov_nat = adjT[:, 3, 0:HALF].bitcast(bf16).rearrange("p (t s r) -> p t s r", s=8, r=R)
        ident_b = adjT[:, 4, 0:P // 2].bitcast(bf16)

        ps = ctx.enter_context(nc.psum_tensor("ps", [P, 8, 512], fp32))

        const_loaded = sem("const_loaded")
        u_loaded = sem("u_loaded")
        wss_cleared = sem("wss_cleared")
        ident_step = sem("ident_step")
        u_split = sem("u_split")
        u_flipped = sem("u_flipped")
        u_ready = sem("u_ready")
        row_loaded = [sem(f"row_loaded{s}") for s in range(SLOTS)]
        x_loaded = sem("x_loaded")
        row_flipped = sem("row_flipped")
        adjT_ready = sem("adjT_ready")
        row_summed = sem("row_summed")
        logits_done = sem("logits_done")
        sigmoid_done = sem("sigmoid_done")
        pool_added = sem("pool_added")
        dve_added = sem("dve_added")
        k_ready = sem("k_ready")
        deg_ready = sem("deg_ready")
        d_ready = sem("d_ready")
        xs_ready = sem("xs_ready")
        k_used = sem("k_used")
        acc_done = sem("acc_done")
        agg_ready = sem("agg_ready")
        hidden_done = sem("hidden_done")
        h_ready = sem("h_ready")
        diag_ready = sem("diag_ready")
        msg_done = sem("msg_done")
        msg_ready = sem("msg_ready")
        post_done = sem("post_done")
        post_read = sem("post_read")
        xT_done = sem("xT_done")
        xT_ready = sem("xT_ready")
        rowsum_ready = sem("rowsum_ready")
        dinv_ready = sem("dinv_ready")
        eye_added = sem("eye_added")
        ys_ready = sem("ys_ready")
        var_ready = sem("var_ready")
        rstd_ready = sem("rstd_ready")
        x_ready = sem("x_ready")
        dve_step = sem("dve_step")
        stored = sem("stored")
        stores_over = sem("stores_over")

        X_L0, X_L1, X_L2, X_L3, X_ALL = 0, NG, 2 * NG, 3 * NG, 4 * NG
        ACC_A, ACC_B, ACC_C, ACC_L2, ACC_L3, ACC_ALL = [i * NG for i in range(6)]
        AGG_L1, AGG_L2, AGG_L3, AGG_ALL = 2, 2 + NG, 2 + 2 * NG, 2 + 3 * NG

        all_rows = adj.rearrange("b n m -> (b n) m")

        def rows_of(b, J):
            at = b * N + J * P
            return all_rows[at:at + P, :] if isinstance(b, int) else all_rows[bass.ds(at, P), :]

        def nodes_of(a, b):
            v = a[b, :, :] if isinstance(b, int) else a[bass.ds(b, 1), :, :].rearrange("a n c -> (a n) c")
            return v.rearrange("(t p) c -> p t c", p=P)

        def T_loaded(b, I):
            return DMA * (b * LOADS + (I // SLOTS + 1))

        def K_loaded(b, J):
            if J >= T - SLOTS:
                return T_loaded(b, J)
            return DMA * (b * LOADS + (T_LOADS + (T - SLOTS - 1 - J) // SLOTS + 1))

        block = ctx.enter_context(nc.Block())

        @block.sync
        def _(sp):
            sp.dma_start(u_nat, U.rearrange("(t p) r -> p t r", p=P)).then_inc(u_loaded, DMA)

            def load_T(b, I):
                if I >= SLOTS:
                    sp.wait_ge(row_flipped, b * 2 * T + 2 * (I - SLOTS + 1))
                    sp.wait_ge(row_summed, b * 2 * T + 2 * (I - SLOTS + 1))
                sp.dma_start(rows[:, I % SLOTS, :], rows_of(b, I)).then_inc(row_loaded[I % SLOTS], DMA)

            def load_K(b, J, src):
                sp.wait_ge(pool_added, b * T + (T - SLOTS - J))
                sp.wait_ge(dve_added, b * T + (T - SLOTS - J))
                sp.dma_start(rows[:, J % SLOTS, :], src).then_inc(row_loaded[J % SLOTS], DMA)

            def store(b, g):
                sp.wait_ge(x_ready, b * X_ALL + (X_L3 + g + 1))
                sp.dma_start(nodes_of(out, b)[:, g * G:(g + 1) * G, :],
                             xb[:, g * G:(g + 1) * G, :]).then_inc(stored, DMA)

            for I in range(SLOTS):
                load_T(0, I)
            sp.wait_ge(wss_cleared, 1)
            for half in range(2):
                sp.dma_start(wss[half * C:(half + 1) * C, half * C:(half + 1) * C], W_self).then_inc(const_loaded, DMA)
            for dst, src in ((w0s, W0), (wns, W_neighbors), (wks, W_l3)):
                for half in range(2):
                    sp.dma_start(dst[half * C:(half + 1) * C, :], src).then_inc(const_loaded, DMA)
            for dst, src in ((w1, W1), (w2, W2), (wout, Wout)):
                sp.dma_start(dst[:, :], src).then_inc(const_loaded, DMA)
            for dst, src in ((b0b, b0), (b1b, b1), (b2b, b2), (boutb, bout)):
                sp.dma_start(dst[:, :], src.partition_broadcast(P)).then_inc(const_loaded, DMA)
            sp.dma_start(biasb[:, :], bias[0, :].partition_broadcast(P)).then_inc(const_loaded, DMA)
            sp.dma_start(wsc[:, :], w_scale.partition_broadcast(P)).then_inc(const_loaded, DMA)
            sp.dma_start(mask[:, :, :], nodemask).then_inc(const_loaded, DMA)
            for g in range(NG):
                sp.dma_start(xa[:, g * G:(g + 1) * G, :],
                             nodes_of(x, 0)[:, g * G:(g + 1) * G, :]).then_inc(x_loaded, DMA)
            for I in range(SLOTS, T):
                load_T(0, I)

            def batch(b, last, after=B):
                for J in range(T - SLOTS - 1, -1, -1):
                    at = after * N - (N - J * P)
                    load_K(b, J, all_rows[at:at + P, :] if last else all_rows[bass.ds(at, P), :])
                if not last:
                    sp.wait_ge(pool_added, b * T + T)
                    sp.wait_ge(dve_added, b * T + T)
                    for I in (1, 2, 3, 0):
                        load_T(b + 1, I)
                    sp.wait_ge(x_ready, b * X_ALL + X_L3)
                    for g in (1, 2, 3, 0):
                        sp.dma_start(xa[:, g * G:(g + 1) * G, :],
                                     nodes_of(x, b + 1)[:, g * G:(g + 1) * G, :]).then_inc(x_loaded, DMA)
                for g in range(NG - 1):
                    if not last:
                        for I in range((g + 1) * G, (g + 2) * G):
                            load_T(b + 1, I)
                    store(b, g)
                store(b, NG - 1)
                sp.wait_ge(stored, (b + 1) * NG * DMA)
                sp.sem_inc(stores_over, 1)

            with sp.Fori(1, B) as after:
                batch(after - 1, False, after)
            batch(B - 1, True)

        @block.tensor
        def _(pe):
            pe.wait_ge(u_split, 1)
            pe.wait_ge(ident_step, 3)
            for side, nat in enumerate((ustat_nat, umov_nat)):
                for q in range(NG):
                    dst = ps[:, side * NG + q, 0:GN // 2].bitcast(bf16)
                    for c in range(G):
                        last = pe.transpose(dst[:, c * P:(c + 1) * P],
                                            nat[:, q * G + c, :, :].rearrange("p s r -> p (s r)"), ident_b)
                    last.then_inc(u_flipped, 1)
            pe.wait_ge(u_ready, 2 * NG)

            def flip_row(b, I):
                pe.wait_ge(row_loaded[I % SLOTS], T_loaded(b, I))
                for h in range(2):
                    if I >= 1:
                        pe.wait_ge(adjT_ready, b * 2 * T + (2 * (I - 1) + h + 1))
                    for j in range(T // 2):
                        last = pe.transpose(ps[:, 4 + 2 * h + j // G, (j % G) * P:(j % G + 1) * P],
                                            rows[:, I % SLOTS, (h * T // 2 + j) * P:(h * T // 2 + j + 1) * P],
                                            ident[:, :])
                    last.then_inc(row_flipped, 1)

            def narrow(bank, g, feats, k):
                for o in range(2):
                    last = pe.matmul(ps[o * C:(o + 1) * C, bank, :], feats[:, k + o, :],
                                     adjT[:, k + o, g * GN:(g + 1) * GN], start=(k == 0), stop=(k + 2 == T))
                return last

            def wide(bank, g, k):
                return pe.matmul(ps[:, bank, :], msg[:, k, :], adjT[:, k, g * GN:(g + 1) * GN],
                                 start=(k == 0), stop=(k + 1 == T))

            def narrow_product(feats, g, bank):
                for k in range(0, T, 2):
                    last = narrow(bank, g, feats, k)
                last.then_inc(acc_done, 1)

            def post(ready, value, lhs, rhs, bank, at=0):
                pe.wait_ge(ready, value)
                for c in range(G):
                    last = pe.matmul(ps[:, bank, at + c * C:at + (c + 1) * C], lhs(c), rhs, start=True, stop=True)
                return last

            def batch(b, is_last):
                def product(i):
                    pe.wait_ge(xs_ready, b * T + (i + 1))
                    for half in range(2):
                        for o in range(2):
                            g = 2 * half + o
                            last = pe.matmul(ps[o * C:(o + 1) * C, half, :], xs[:, i % 2, :],
                                             work[:, i % 3, g * GN:(g + 1) * GN],
                                             start=(i == 0), stop=(i + 1 == T))
                    last.then_inc(k_used, 1)

                pe.wait_ge(adjT_ready, b * 2 * T + 2 * T)
                for i in range(T):
                    J = T - 1 - i
                    if i >= 2:
                        product(i - 2)
                    for q in range(NG):
                        if i >= 1 and q % 2 == 0:
                            pe.wait_ge(k_ready, b * 2 * T + (2 * (i - 1) + q // 2 + 1))
                        last = pe.matmul(ps[:, 4 + q, :], ustat[:, J * P:(J + 1) * P], umov[:, q * GN:(q + 1) * GN],
                                         start=True, stop=True)
                        if q % 2 == 1:
                            last.then_inc(logits_done, 1)
                product(T - 2)
                product(T - 1)
                for half in range(2):
                    pe.wait_ge(agg_ready, b * AGG_ALL + (half + 1))
                    for c in range(G):
                        last = pe.transpose(ps[:, 2 + half, c * P:(c + 1) * P], agg[:, half, c * P:(c + 1) * P],
                                            ident[:, :])
                    last.then_inc(post_done, 2)

                def first_two(ready, base, feats, tail):
                    for q in range(NG):
                        pe.wait_ge(ready, base + (q + 1))
                        for g in range(2):
                            for k in range(q * G, (q + 1) * G, 2):
                                last = narrow(g, g, feats, k)
                            if q == NG - 1:
                                last.then_inc(acc_done, 1)
                        if q == 0:
                            tail()

                def hidden(g):
                    pe.wait_ge(agg_ready, b * AGG_ALL + (AGG_L1 + g + 1))
                    pe.wait_ge(diag_ready, b * NG + (g + 1))
                    if g >= 2:
                        pe.wait_ge(h_ready, b * 3 * NG + (g - 1))
                    pe.matmul(ps[:, 4 + g % 2, :], w0s[:, :], agg[:, g % 2, :], start=True, stop=False)
                    pe.matmul(ps[:, 4 + g % 2, :], b0b[:, :], diag[:, g % 2, :],
                              start=False, stop=True).then_inc(hidden_done, 1)

                def message(layer, g, w):
                    pe.wait_ge(h_ready, b * 3 * NG + (layer * NG + g + 1))
                    if g >= 2:
                        pe.wait_ge(msg_ready, b * 2 * NG + (layer * NG + g - 1))
                    for c in range(G):
                        t = g * G + c
                        last = pe.matmul(ps[:, 6 + g % 2, c * HID:(c + 1) * HID], hT[:, t * P:(t + 1) * P], w[:, :],
                                         start=True, stop=True)
                    last.then_inc(msg_done, 1)

                first_two(x_ready, b * X_ALL + X_L0, xa, lambda: None)
                narrow_product(xa, 2, 2)
                hidden(0)
                hidden(1)
                narrow_product(xa, 3, 3)
                hidden(2)
                message(0, 0, w1)
                message(0, 1, w1)
                hidden(3)
                message(0, 2, w1)
                message(0, 3, w1)

                for layer in range(2):
                    for q in range(NG):
                        pe.wait_ge(msg_ready, b * 2 * NG + (layer * NG + q + 1))
                        for g in range(2):
                            for k in range(q * G, (q + 1) * G):
                                last = wide(g, g, k)
                            if q == NG - 1:
                                last.then_inc(acc_done, 1)
                    for g in range(2, NG):
                        for k in range(T):
                            last = wide(g, g, k)
                        last.then_inc(acc_done, 1)
                        if layer == 1 and g == 2:
                            for gg in range(2):
                                out_layer(pe, b, gg)
                    if layer == 0:
                        for g in range(NG):
                            message(1, g, w2)
                out_layer(pe, b, 2)

                first_two(x_ready, b * X_ALL + X_L1, xa, lambda: out_layer(pe, b, 3))
                for v in range(2):
                    for u in range(v * G, (v + 1) * G):
                        last = pe.transpose(ps[:, 6 + v, (u % G) * P:(u % G + 1) * P],
                                            xa[:, 2 * u:2 * u + 2, :].rearrange("p t c -> p (t c)"), ident[:, :])
                    last.then_inc(xT_done, 1)

                def post_L2(g):
                    if g >= 2:
                        pe.wait_ge(post_read, b * X_ALL + (X_L2 + g - 1))
                    pe.wait_ge(xT_ready, b * 2 + (g // 2 + 1))
                    for v in range(G // 2):
                        pe.matmul(ps[:, 4 + g % 2, (G + 2 * v) * C:(G + 2 * v + 2) * C],
                                  xT[:, g * G // 2 + v, :], wss[:, :], start=True, stop=True)
                    post(agg_ready, b * AGG_ALL + (AGG_L2 + g + 1), lambda c: agg[:, g % 2, c * P:(c + 1) * P],
                         wns[:, :], 4 + g % 2).then_inc(post_done, 1)

                narrow_product(xa, 2, 2)
                post_L2(0)
                post_L2(1)
                for k in range(0, T, 2):
                    last = narrow(3, 3, xa, k)
                    if k == G * 2:
                        post_L2(2)
                last.then_inc(acc_done, 1)

                def post_L3(g):
                    if g >= 1:
                        pe.wait_ge(post_read, b * X_ALL + (X_L3 + g))
                    post(agg_ready, b * AGG_ALL + (AGG_L3 + g + 1), lambda c: agg[:, g % 2, c * P:(c + 1) * P],
                         wks[:, :], 3).then_inc(post_done, 1)

                for g in range(NG):
                    pe.wait_ge(eye_added, b * NG + (g + 1))
                    for k in range(0, T, 2):
                        if g == 0 and k % G == 0:
                            pe.wait_ge(ys_ready, b * NG + (k // G + 1))
                        last = narrow(g % 3, g, ys, k)
                        if k + 2 == T:
                            last.then_inc(acc_done, 1)
                        if g == 0 and k + 2 == G:
                            post_L2(3)
                        if g >= 1 and k % 4 == 2 and not is_last:
                            flip_row(b + 1, (g - 1) * G + k // 4)
                    if g >= 1:
                        post_L3(g - 1)
                for c in range(G):
                    if not is_last:
                        flip_row(b + 1, (NG - 1) * G + c)
                    if c == 0:
                        post_L3(NG - 1)

            def out_layer(pe, b, g):
                if g >= 2:
                    pe.wait_ge(post_read, b * X_ALL + (X_L1 + g - 1))
                post(h_ready, b * 3 * NG + (2 * NG + g + 1), lambda c: hT[:, (g * G + c) * P:(g * G + c + 1) * P],
                     wout[:, :], 4 + g % 2).then_inc(post_done, 1)

            for I in range(T):
                flip_row(0, I)
            pe.wait_ge(const_loaded, CONSTS * DMA)
            with pe.Fori(0, B - 1) as b:
                batch(b, False)
            batch(B - 1, True)

        @block.scalar
        def _(act):
            for side, dst in enumerate((ustat, umov)):
                for q in range(NG):
                    act.wait_ge(u_flipped, side * NG + q + 1)
                    act.activation(dst[:, q * GN:(q + 1) * GN], ps[:, side * NG + q, 0:GN // 2].bitcast(bf16),
                                   ACT.Copy).then_inc(u_ready, 1)

            def keep_row(b, I):
                for h in range(2):
                    act.wait_ge(row_flipped, b * 2 * T + (2 * I + h + 1))
                    act.activation(adjT[:, h * T // 2:(h + 1) * T // 2, I * P:(I + 1) * P],
                                   ps[:, 4 + 2 * h:6 + 2 * h, :].rearrange("p a (j n) -> p (a j) n", n=P),
                                   ACT.Copy).then_inc(adjT_ready, 1)

            def batch(b, is_last):
                for i in range(T):
                    for h in range(2):
                        act.wait_ge(logits_done, b * 2 * T + (2 * i + h + 1))
                        act.activation(ps[:, 4 + 2 * h:6 + 2 * h, :], ps[:, 4 + 2 * h:6 + 2 * h, :],
                                       ACT.Sigmoid).then_inc(sigmoid_done, 1)
                act.wait_ge(k_used, b * T + T)
                for half in range(2):
                    act.activation(agg[:, half, :], ps[:, half, :], ACT.Copy).then_inc(agg_ready, 1)

                def keep_agg(acc, g, bank):
                    act.wait_ge(acc_done, b * ACC_ALL + (acc + g + 1))
                    act.activation(agg[:, g % 2, :], ps[:, bank, :], ACT.Copy).then_inc(agg_ready, 1)

                def relu(src, g):
                    act.activation(hT[:, g * GN:(g + 1) * GN], ps[:, src, :], ACT.Relu).then_inc(h_ready, 1)

                keep_agg(ACC_A, 0, 0)
                keep_agg(ACC_A, 1, 1)
                for g in range(2):
                    act.wait_ge(hidden_done, b * NG + (g + 1))
                    relu(4 + g, g)
                keep_agg(ACC_A, 2, 2)
                keep_agg(ACC_A, 3, 3)
                for g in range(2, NG):
                    act.wait_ge(hidden_done, b * NG + (g + 1))
                    relu(4 + g % 2, g)
                for acc in (ACC_B, ACC_C):
                    for g in range(NG):
                        act.wait_ge(acc_done, b * ACC_ALL + (acc + g + 1))
                        relu(g, g)
                keep_agg(ACC_L2, 0, 0)
                keep_agg(ACC_L2, 1, 1)
                for v in range(2):
                    act.wait_ge(xT_done, b * 2 + (v + 1))
                    act.activation(xT[:, v * G:(v + 1) * G, :], ps[:, 6 + v, :].rearrange("p (u n) -> p u n", n=P),
                                   ACT.Copy).then_inc(xT_ready, 1)
                for g in range(2, NG):
                    act.wait_ge(post_done, b * X_ALL + (X_L2 + g - 1))
                    keep_agg(ACC_L2, g, g)
                for g in range(NG):
                    if g >= 2:
                        act.wait_ge(post_done, b * X_ALL + (X_L3 + g - 1))
                    keep_agg(ACC_L3, g, g % 3)
                    if not is_last:
                        for I in range(g * G, (g + 1) * G):
                            keep_row(b + 1, I)

            for I in range(T):
                keep_row(0, I)
            with act.Fori(0, B - 1) as b:
                batch(b, False)
            batch(B - 1, True)

        @block.vector
        def _(dve):
            steps = [0]

            def link(instruction):
                steps[0] += 1
                instruction.then_inc(dve_step, 1)
                dve.wait_ge(dve_step, steps[0])

            def restart():
                dve.sem_clear(dve_step)
                steps[0] = 0

            parts = ((1, 1, 2, 2, 1, 3, 2, 3), (1, 2, 1, 2, 3, 1, 3, 2))
            dve.wait_ge(u_loaded, DMA)
            src = u_nat
            for part in (1, 2, 3):
                for side, nat in enumerate((ustat_nat, umov_nat)):
                    for s in range(8):
                        if parts[side][s] == part:
                            link(dve.tensor_copy(nat[:, :, s, :], src))
                if part < 3:
                    s = parts[0].index(part)
                    link(dve.tensor_sub(u_rest, src, ustat_nat[:, :, s, :]))
                    src = u_rest
            dve.memset(neghalf[:, :], -0.5).then_inc(u_split, 1)
            restart()

            def sum_row(b, I):
                dve.wait_ge(row_loaded[I % SLOTS], T_loaded(b, I))
                dve.reduce_sum(rowsum[:, I:I + 1], rows[:, I % SLOTS, :], X).then_inc(row_summed, 2)

            def over(stat):
                return stat.unsqueeze(2).to_broadcast([P, G, C])

            def layer_norm(b, base, g, dst):
                link(dve.reduce_sum(total[:, :], yv, X))
                link(dve.scalar_tensor_tensor(yv, over(total[:, :]), -1.0 / C, yv, ALU.mult, ALU.add))
                link(dve.tensor_mul(sq, yv, yv))
                link(dve.reduce_sum(var[:, :], sq, X))
                dve.tensor_scalar(var[:, :], var[:, :], 1.0 / C, LN_EPS, ALU.mult, ALU.add).then_inc(var_ready, 1)
                dve.wait_ge(rstd_ready, b * X_ALL + (base + g + 1))
                dve.tensor_mul(dst[:, g * G:(g + 1) * G, :], yv, over(rstd[:, :])).then_inc(x_ready, 1)
                dve.wait_ge(x_ready, b * X_ALL + (base + g + 1))

            def batch(b, is_last):
                def add_row(i):
                    J = T - 1 - i
                    if i == 0:
                        dve.wait_ge(adjT_ready, b * 2 * T + 2 * T)
                    if i >= 3:
                        dve.wait_ge(k_used, b * T + (i - 2))
                    dve.wait_ge(row_loaded[J % SLOTS], K_loaded(b, J))
                    dve.tensor_add(work[:, i % 3, POOL_COLS:N], rows[:, J % SLOTS, POOL_COLS:N],
                                   adjT[:, J, POOL_COLS:N]).then_inc(dve_added, 1)

                add_row(0)
                for i in range(T):
                    J = T - 1 - i
                    if i + 1 < T:
                        add_row(i + 1)
                    dve.wait_ge(pool_added, b * T + (i + 1))
                    dve.wait_ge(dve_added, b * T + (i + 1))
                    for h in range(2):
                        dve.wait_ge(sigmoid_done, b * 2 * T + (2 * i + h + 1))
                        part = work[:, i % 3, h * HALF:(h + 1) * HALF]
                        dve.scalar_tensor_tensor(part, ps[:, 4 + 2 * h:6 + 2 * h, :].rearrange("p a n -> p (a n)"),
                                                 0.5, part, ALU.mult, ALU.mult,
                                                 accum_out=kpart[:, J, h:h + 1]).then_inc(k_ready, 1)
                    dve.wait_ge(k_ready, b * 2 * T + (2 * i + 2))
                    dve.tensor_scalar(deg[:, J:J + 1], kpart[:, J, 0:1], kpart[:, J, 1:2], DEG_EPS,
                                      ALU.add, ALU.max).then_inc(deg_ready, 1)
                dve.wait_ge(d_ready, b * T + T)
                if b is not None:
                    dve.wait_ge(const_loaded, CONSTS * DMA)
                link(dve.tensor_scalar(dw[:, :], dl0[:, :], wsc[:, :], None, ALU.mult))

                def result(base, g, bank):
                    dve.wait_ge(post_done, b * X_ALL + (base + g + 1))
                    return ps[:, bank, 0:G * C].rearrange("p (t c) -> p t c", c=C)

                def seen(base, g):
                    dve.wait_ge(post_read, b * X_ALL + (base + g + 1))

                def grp(a, g):
                    return a[:, g * G:(g + 1) * G]

                for g in range(NG):
                    dve.wait_ge(post_done, b * X_ALL + (X_L0 + g + 1))
                    r = ps[:, 2 + g // 2, :].rearrange("p (t o c) -> p t o c", o=2, c=C)[:, :, g % 2, :]
                    dve.tensor_mul(yv, r, over(grp(dw, g))).then_inc(post_read, 1)
                    seen(X_L0, g)
                    link(dve.tensor_add(yv, yv, xa[:, g * G:(g + 1) * G, :]))
                    layer_norm(b, X_L0, g, xa)

                def diag_of(g):
                    if g >= 2:
                        dve.wait_ge(hidden_done, b * NG + (g - 1))
                    dve.tensor_mul(diag[:, g % 2, :].rearrange("p (t n) -> p t n", n=P),
                                   ident[:, :].unsqueeze(1).to_broadcast([P, G, P]),
                                   grp(rowsum, g).unsqueeze(2).to_broadcast([P, G, P])).then_inc(diag_ready, 1)

                def sum_columns(lo, hi):
                    for j in range(lo, hi):
                        last = dve.reduce_sum(colsum[:, j:j + 1], adjT[:, j, :], X)
                    return last

                def keep_message(layer, g, biases):
                    dve.wait_ge(msg_done, b * 2 * NG + (layer * NG + g + 1))
                    dve.tensor_add(msg[:, g * G:(g + 1) * G, :], ps[:, 6 + g % 2, :].rearrange("p (t d) -> p t d", d=HID),
                                   biases[:, :].unsqueeze(1).to_broadcast([P, G, HID])).then_inc(msg_ready, 1)

                diag_of(0)
                diag_of(1)
                sum_columns(0, 5)
                diag_of(2)
                diag_of(3)
                for g in range(NG):
                    keep_message(0, g, b1b)
                sum_columns(5, T - 1)
                link(sum_columns(T - 1, T))
                zero, safe, keep = tiny[:, 0, :], tiny[:, 1, :], tiny[:, 2, :]
                link(dve.tensor_scalar(zero, colsum[:, :], 0.0, None, ALU.is_equal))
                link(dve.tensor_add(safe, colsum[:, :], zero))
                link(dve.reciprocal(safe, safe))
                link(dve.tensor_scalar(keep, zero, -1.0, 1.0, ALU.mult, ALU.add))
                link(dve.tensor_mul(invdeg[:, :], safe, keep))
                link(dve.tensor_scalar(safe, rowsum[:, :], 1.0, None, ALU.add))
                link(dve.tensor_scalar(keep, safe, 0.0, None, ALU.is_gt))
                dve.tensor_scalar(safe, safe, 1e-37, None, ALU.max).then_inc(rowsum_ready, 1)
                dve.wait_ge(dinv_ready, b + 1)
                link(dve.tensor_mul(dinv[:, :], dinv[:, :], keep))
                dve.wait_ge(acc_done, b * ACC_ALL + (ACC_B + NG))
                for g in range(NG):
                    keep_message(1, g, b2b)
                mask_b = mask[:, b, :] if isinstance(b, int) else \
                    mask[:, bass.ds(b, 1), :].rearrange("p a t -> p (a t)")
                for g in range(NG):
                    r = result(X_L1, g, 4 + g % 2)
                    dve.tensor_add(yv, r, boutb[:, :].unsqueeze(1).to_broadcast([P, G, C])).then_inc(post_read, 1)
                    seen(X_L1, g)
                    link(dve.tensor_mul(yv, yv, over(grp(mask_b, g))))
                    link(dve.tensor_add(yv, yv, xa[:, g * G:(g + 1) * G, :]))
                    layer_norm(b, X_L1, g, xa)

                for g in range(NG):
                    r = result(X_L2, g, 4 + g % 2)
                    link(dve.tensor_mul(yv, r, over(grp(invdeg, g))))
                    dve.tensor_add(yv, yv, ps[:, 4 + g % 2, G * C:2 * G * C].rearrange("p (t c) -> p t c", c=C))\
                       .then_inc(post_read, 1)
                    seen(X_L2, g)
                    link(dve.tensor_add(yv, yv, xa[:, g * G:(g + 1) * G, :]))
                    link(dve.tensor_add(yv, yv, biasb[:, :].unsqueeze(1).to_broadcast([P, G, C])))
                    layer_norm(b, X_L2, g, xb)
                    dve.tensor_mul(ys[:, g * G:(g + 1) * G, :], xb[:, g * G:(g + 1) * G, :], over(grp(dinv, g)))\
                       .then_inc(ys_ready, 1)
                    dve.wait_ge(acc_done, b * ACC_ALL + (ACC_L2 + g + 1))
                    for k in range(g * G, (g + 1) * G):
                        block_kk = adjT_flat[:, k * (N + P):k * (N + P) + P]
                        last = dve.tensor_add(block_kk, block_kk, ident[:, :])
                    last.then_inc(eye_added, 1)

                for g in range(NG):
                    if g >= 1 and not is_last:
                        for I in range((g - 1) * G, g * G):
                            sum_row(b + 1, I)
                    if g == 0:
                        continue
                    post_L3(b, g - 1, result, seen, grp)
                if not is_last:
                    sum_row(b + 1, (NG - 1) * G)
                post_L3(b, NG - 1, result, seen, grp)
                if not is_last:
                    for I in range((NG - 1) * G + 1, T):
                        sum_row(b + 1, I)
                restart()

            def post_L3(b, g, result, seen, grp):
                r = result(X_L3, g, 3)
                dve.tensor_mul(yv, r, over(grp(dinv, g))).then_inc(post_read, 1)
                seen(X_L3, g)
                link(dve.scalar_tensor_tensor(yv, yv, 0.0, xb[:, g * G:(g + 1) * G, :], ALU.max, ALU.add))
                layer_norm(b, X_L3, g, xb)

            for I in range(T):
                sum_row(0, I)
            with dve.Fori(0, B - 1) as b:
                batch(b, False)
            batch(B - 1, True)

        @block.gpsimd
        def _(pool):
            pool.memset(wss[:, :], 0.0).then_inc(wss_cleared, 1)
            pool.memset(ident[:, :], 0.0).then_inc(ident_step, 1)
            pool.wait_ge(ident_step, 1)
            pool.affine_select(out=ident[:, :], in_=ident[:, :], compare_op=ALU.not_equal, fill=1.0, base=0,
                               pattern=[[-1, P]], channel_multiplier=1).then_inc(ident_step, 1)
            pool.wait_ge(ident_step, 2)
            pool.tensor_copy(ident_b, ident[:, :]).then_inc(ident_step, 1)

            def power(dst, base, cols, done):
                pool.tensor_tensor(dst, base, neghalf[:, 0:cols], ALU.pow).then_inc(done, 1)

            def batch(b, is_last):
                def add_row(i):
                    J = T - 1 - i
                    if i >= 3:
                        pool.wait_ge(k_used, b * T + (i - 2))
                    pool.wait_ge(row_loaded[J % SLOTS], K_loaded(b, J))
                    pool.tensor_add(work[:, i % 3, 0:POOL_COLS], rows[:, J % SLOTS, 0:POOL_COLS],
                                    adjT[:, J, 0:POOL_COLS]).then_inc(pool_added, 1)

                pool.wait_ge(adjT_ready, b * 2 * T + 2 * T)
                add_row(0)
                add_row(1)
                pool.wait_ge(x_loaded, (b + 1) * (NG * DMA))
                for i in range(T):
                    J = T - 1 - i
                    pool.wait_ge(deg_ready, b * T + (i + 1))
                    power(dl0[:, J:J + 1], deg[:, J:J + 1], 1, d_ready)
                    pool.wait_ge(d_ready, b * T + (i + 1))
                    if i >= 2:
                        pool.wait_ge(k_used, b * T + (i - 1))
                    pool.tensor_mul(xs[:, i % 2, :], xa[:, J, :], dl0[:, J:J + 1].to_broadcast([P, C]))\
                        .then_inc(xs_ready, 1)
                    if i + 2 < T:
                        add_row(i + 2)

                def norm(base, g):
                    pool.wait_ge(var_ready, b * X_ALL + (base + g + 1))
                    power(rstd[:, :], var[:, :], G, rstd_ready)

                for g in range(NG):
                    norm(X_L0, g)
                pool.wait_ge(rowsum_ready, b + 1)
                power(dinv[:, :], tiny[:, 1, :], T, dinv_ready)
                for base in (X_L1, X_L2, X_L3):
                    for g in range(NG):
                        norm(base, g)

            pool.wait_ge(u_split, 1)
            with pool.Fori(0, B - 1) as b:
                batch(b, False)
            batch(B - 1, True)


CONSTS = 8 + 3 + 4 + 2 + 1


_INS = ['x', 'adj', 'nodemask', 'L0_gnn_U', 'L0_gnn_w_scale', 'L1_gnn_W0', 'L1_gnn_b0', 'L1_gnn_W1', 'L1_gnn_b1',
        'L1_gnn_W2', 'L1_gnn_b2', 'L1_gnn_Wout', 'L1_gnn_bout', 'L2_gnn_W_neighbors', 'L2_gnn_W_self',
        'L2_gnn_bias', 'L3_gnn_kernel']


def kernel(**inputs):
    import concourse.bacc as _bacc
    from concourse.bass_utils import run_bass_kernel_spmd as _run

    nc = _bacc.Bacc("TRN2", target_bir_lowering=False, num_devices=1)
    arrays, args = {}, []
    for name in _INS:
        a = np.ascontiguousarray(inputs[name])
        if a.ndim == 0:
            a = a.reshape(1)
        if name == 'nodemask':
            a = np.ascontiguousarray(a.reshape(a.shape[0], -1, 128).transpose(2, 0, 1))
        arrays[f"in_{name}"] = a
        args.append(nc.dram_tensor(f"in_{name}", a.shape, mybir.dt.from_np(a.dtype), kind="ExternalInput").ap())
    shape = inputs['x'].shape
    args.append(nc.dram_tensor("out_x", shape, mybir.dt.float32, kind="ExternalOutput").ap())
    adjacency_stack_kernel(nc, *args)
    r = _run(nc, [arrays], core_ids=[0])
    return r.results[0]["out_x"]
```

```python
from contextlib import ExitStack

import numpy as np

import concourse.bass as bass
from concourse import mybir


def adjacency_stack_kernel(
    nc: bass.Bass,
    x: bass.AP,
    adj: bass.AP,
    nodemask: bass.AP,
    U: bass.AP,
    w_scale: bass.AP,
    W0: bass.AP,
    b0: bass.AP,
    W1: bass.AP,
    b1: bass.AP,
    W2: bass.AP,
    b2: bass.AP,
    Wout: bass.AP,
    bout: bass.AP,
    W_neighbors: bass.AP,
    W_self: bass.AP,
    bias: bass.AP,
    W_l3: bass.AP,
    out: bass.AP,
):
    fp32 = mybir.dt.float32
    bf16 = mybir.dt.bfloat16
    ALU = mybir.AluOpType
    ACT = mybir.ActivationFunctionType
    X = mybir.AxisListType.X

    B, N, C = x.shape
    HID = W1.shape[0]
    R = U.shape[1]
    P = 128
    T = N // P
    G = 4
    NG = T // G
    GN = G * P
    SLOTS = 4
    T_LOADS = T // SLOTS
    K_LOADS = (T - SLOTS) // SLOTS
    LOADS = T_LOADS + K_LOADS
    DMA = 16
    POOL_COLS = [704] + [1216] * (T - 1)
    DEG_EPS = 1e-12
    LN_EPS = 1e-5
    HALF = N // 2
    assert P == 2 * C and HID == P and T == 16 and NG == 4

    with ExitStack() as ctx:
        def sb(name, shape, dt=fp32):
            return ctx.enter_context(nc.sbuf_tensor(name, shape, dt))

        def sem(name):
            return ctx.enter_context(nc.semaphore(name))

        adjT = sb("adjT", [P, T, N])
        rows = sb("rows", [P, SLOTS, N])
        work = sb("work", [P, 3, N])
        ustat = sb("ustat", [P, N], bf16)
        umov = sb("umov", [P, N], bf16)
        xa = sb("xa", [P, T, C])
        xb = sb("xb", [P, T, C])
        w0s = sb("w0s", [P, HID])
        w1 = sb("w1", [P, HID])
        w2 = sb("w2", [P, HID])
        wout = sb("wout", [P, C])
        wns = sb("wns", [P, C])
        wss = sb("wss", [P, P])
        wks = sb("wks", [P, C])
        ident = sb("ident", [P, P])
        b0b = sb("b0b", [P, HID])
        b1b = sb("b1b", [P, HID])
        b2b = sb("b2b", [P, HID])
        boutb = sb("boutb", [P, C])
        biasb = sb("biasb", [P, C])
        wsc = sb("wsc", [P, 1])
        mask = sb("mask", [P, B, T])
        neghalf = sb("neghalf", [P, T])
        rowpart = sb("rowpart", [P, 2, T])
        rowsum = sb("rowsum", [P, T])
        colsum = sb("colsum", [P, T])
        kpart = sb("kpart", [P, T, 2])
        deg = sb("deg", [P, T])
        dl0 = sb("dl0", [P, T])
        dw = sb("dw", [P, T])
        invdeg = sb("invdeg", [P, T])
        dinv = sb("dinv", [P, T])
        tiny = sb("tiny", [P, 3, T])
        stats = sb("stats", [P, G, 6])
        moments = sb("moments", [P, G, 2])
        var = sb("var", [P, G])
        rstd = sb("rstd", [P, G])
        xs = sb("xs", [P, 2, C])

        hT = work[:, 0, :]
        ys = work[:, 0, T * C:2 * T * C].rearrange("p (t c) -> p t c", c=C)
        msg = work[:, 1, :].rearrange("p (t d) -> p t d", d=HID)
        xT = work[:, 1, 0:T * C].rearrange("p (u n) -> p u n", n=P)
        agg = work[:, 2, 0:2 * GN].rearrange("p (s n) -> p s n", n=GN)
        yv = [work[:, 2, 1024 + i * 256:1280 + i * 256].rearrange("p (t c) -> p t c", c=C) for i in range(2)]
        x1m = xb
        x2b = work[:, 0, 0:T * C].rearrange("p (t c) -> p t c", c=C)
        diag = xb[:, :, :].rearrange("p (s t) c -> p s (t c)", s=2)
        adjT_flat = adjT[:, :, :].rearrange("p j i -> p (j i)")

        u_nat = adjT[:, 0, 0:T * R].rearrange("p (t r) -> p t r", r=R)
        u_rest = adjT[:, 1, 0:T * R].rearrange("p (t r) -> p t r", r=R)
        ustat_nat = adjT[:, 2, 0:HALF].bitcast(bf16).rearrange("p (t s r) -> p t s r", s=8, r=R)
        umov_nat = adjT[:, 3, 0:HALF].bitcast(bf16).rearrange("p (t s r) -> p t s r", s=8, r=R)
        ident_b = adjT[:, 4, 0:P // 2].bitcast(bf16)

        ps = ctx.enter_context(nc.psum_tensor("ps", [P, 8, 512], fp32))

        const_loaded = sem("const_loaded")
        u_loaded = sem("u_loaded")
        wss_cleared = sem("wss_cleared")
        ident_step = sem("ident_step")
        u_split = sem("u_split")
        u_flipped = sem("u_flipped")
        u_ready = sem("u_ready")
        row_loaded = [sem(f"row_loaded{s}") for s in range(SLOTS)]
        x_loaded = sem("x_loaded")
        row_flipped = sem("row_flipped")
        adjT_ready = sem("adjT_ready")
        row_summed = sem("row_summed")
        half_summed = sem("half_summed")
        logits_done = sem("logits_done")
        sigmoid_done = sem("sigmoid_done")
        pool_added = sem("pool_added")
        dve_added = sem("dve_added")
        k_ready = sem("k_ready")
        deg_ready = sem("deg_ready")
        d_ready = sem("d_ready")
        xs_ready = sem("xs_ready")
        k_used = sem("k_used")
        acc_done = sem("acc_done")
        agg_ready = sem("agg_ready")
        hidden_done = sem("hidden_done")
        h_ready = sem("h_ready")
        diag_ready = sem("diag_ready")
        msg_done = sem("msg_done")
        msg_ready = sem("msg_ready")
        post_done = sem("post_done")
        post_read = sem("post_read")
        xT_done = sem("xT_done")
        xT_ready = sem("xT_ready")
        rowsum_ready = sem("rowsum_ready")
        dinv_ready = sem("dinv_ready")
        dinv_set = sem("dinv_set")
        bout_masked = sem("bout_masked")
        x1m_ready = sem("x1m_ready")
        x2b_ready = sem("x2b_ready")
        eye_added = sem("eye_added")
        ys_ready = sem("ys_ready")
        var_ready = sem("var_ready")
        rstd_ready = sem("rstd_ready")
        x_ready = sem("x_ready")
        dve_step = sem("dve_step")
        stored = sem("stored")
        stores_over = sem("stores_over")

        X_L0, X_L1, X_L2, X_L3, X_ALL = 0, NG, 2 * NG, 3 * NG, 4 * NG
        ACC_A, ACC_B, ACC_C, ACC_L2, ACC_L3, ACC_ALL = [i * NG for i in range(6)]
        AGG_L1, AGG_L2, AGG_L3, AGG_ALL = 2, 2 + NG, 2 + 2 * NG, 2 + 3 * NG

        all_rows = adj.rearrange("b n m -> (b n) m")

        def rows_of(b, J):
            at = b * N + J * P
            return all_rows[at:at + P, :] if isinstance(b, int) else all_rows[bass.ds(at, P), :]

        def nodes_of(a, b):
            v = a[b, :, :] if isinstance(b, int) else a[bass.ds(b, 1), :, :].rearrange("a n c -> (a n) c")
            return v.rearrange("(t p) c -> p t c", p=P)

        def T_loaded(b, I):
            return DMA * (b * LOADS + (I // SLOTS + 1))

        def K_loaded(b, J):
            if J >= T - SLOTS:
                return T_loaded(b, J)
            return DMA * (b * LOADS + (T_LOADS + (T - SLOTS - 1 - J) // SLOTS + 1))

        block = ctx.enter_context(nc.Block())

        @block.sync
        def _(sp):
            sp.dma_start(u_nat, U.rearrange("(t p) r -> p t r", p=P)).then_inc(u_loaded, DMA)

            def load_T(b, I):
                if I >= SLOTS:
                    sp.wait_ge(row_flipped, b * 2 * T + 2 * (I - SLOTS + 1))
                    sp.wait_ge(row_summed, b * 2 * T + 2 * (I - SLOTS + 1))
                sp.dma_start(rows[:, I % SLOTS, :], rows_of(b, I)).then_inc(row_loaded[I % SLOTS], DMA)

            def load_K(b, J, src):
                sp.wait_ge(pool_added, b * T + (T - SLOTS - J))
                sp.wait_ge(dve_added, b * T + (T - SLOTS - J))
                sp.wait_ge(half_summed, b * T + (T - SLOTS - J))
                sp.dma_start(rows[:, J % SLOTS, :], src).then_inc(row_loaded[J % SLOTS], DMA)

            def store(b, g):
                sp.wait_ge(x_ready, b * X_ALL + (X_L3 + g + 1))
                sp.dma_start(nodes_of(out, b)[:, g * G:(g + 1) * G, :],
                             xb[:, g * G:(g + 1) * G, :]).then_inc(stored, DMA)

            for I in range(SLOTS):
                load_T(0, I)
            sp.wait_ge(wss_cleared, 1)
            for half in range(2):
                sp.dma_start(wss[half * C:(half + 1) * C, half * C:(half + 1) * C], W_self).then_inc(const_loaded, DMA)
            for dst, src in ((w0s, W0), (wns, W_neighbors), (wks, W_l3)):
                for half in range(2):
                    sp.dma_start(dst[half * C:(half + 1) * C, :], src).then_inc(const_loaded, DMA)
            for dst, src in ((w1, W1), (w2, W2), (wout, Wout)):
                sp.dma_start(dst[:, :], src).then_inc(const_loaded, DMA)
            for dst, src in ((b0b, b0), (b1b, b1), (b2b, b2), (boutb, bout)):
                sp.dma_start(dst[:, :], src.partition_broadcast(P)).then_inc(const_loaded, DMA)
            sp.dma_start(biasb[:, :], bias[0, :].partition_broadcast(P)).then_inc(const_loaded, DMA)
            sp.dma_start(wsc[:, :], w_scale.partition_broadcast(P)).then_inc(const_loaded, DMA)
            sp.dma_start(mask[:, :, :], nodemask).then_inc(const_loaded, DMA)
            for g in range(NG):
                sp.dma_start(xa[:, g * G:(g + 1) * G, :],
                             nodes_of(x, 0)[:, g * G:(g + 1) * G, :]).then_inc(x_loaded, DMA)
            for I in range(SLOTS, T):
                load_T(0, I)

            def batch(b, last, after=B):
                for J in range(T - SLOTS - 1, -1, -1):
                    at = after * N - (N - J * P)
                    load_K(b, J, all_rows[at:at + P, :] if last else all_rows[bass.ds(at, P), :])
                if not last:
                    sp.wait_ge(pool_added, b * T + T)
                    sp.wait_ge(dve_added, b * T + T)
                    sp.wait_ge(half_summed, b * T + T)
                    for I in (1, 2, 3, 0):
                        load_T(b + 1, I)
                    sp.wait_ge(x_ready, b * X_ALL + X_L3)
                    for g in (1, 2, 3, 0):
                        sp.dma_start(xa[:, g * G:(g + 1) * G, :],
                                     nodes_of(x, b + 1)[:, g * G:(g + 1) * G, :]).then_inc(x_loaded, DMA)
                for g in range(NG - 1):
                    if not last:
                        for I in range((g + 1) * G, (g + 2) * G):
                            load_T(b + 1, I)
                    store(b, g)
                store(b, NG - 1)
                sp.wait_ge(stored, (b + 1) * NG * DMA)
                sp.sem_inc(stores_over, 1)

            with sp.Fori(1, B) as after:
                batch(after - 1, False, after)
            batch(B - 1, True)

        @block.tensor
        def _(pe):
            pe.wait_ge(u_split, 1)
            pe.wait_ge(ident_step, 3)
            for side, nat in enumerate((ustat_nat, umov_nat)):
                for q in range(NG):
                    dst = ps[:, side * NG + q, 0:GN // 2].bitcast(bf16)
                    for c in range(G):
                        last = pe.transpose(dst[:, c * P:(c + 1) * P],
                                            nat[:, q * G + c, :, :].rearrange("p s r -> p (s r)"), ident_b)
                    last.then_inc(u_flipped, 1)
            pe.wait_ge(u_ready, 2 * NG)

            def flip_row(b, I):
                pe.wait_ge(row_loaded[I % SLOTS], T_loaded(b, I))
                for h in range(2):
                    if I >= 1:
                        pe.wait_ge(adjT_ready, b * 2 * T + (2 * (I - 1) + h + 1))
                    for j in range(T // 2):
                        last = pe.transpose(ps[:, 4 + 2 * h + j // G, (j % G) * P:(j % G + 1) * P],
                                            rows[:, I % SLOTS, (h * T // 2 + j) * P:(h * T // 2 + j + 1) * P],
                                            ident[:, :])
                    last.then_inc(row_flipped, 1)

            def narrow(bank, g, feats, k):
                for o in range(2):
                    last = pe.matmul(ps[o * C:(o + 1) * C, bank, :], feats[:, k + o, :],
                                     adjT[:, k + o, g * GN:(g + 1) * GN], start=(k == 0), stop=(k + 2 == T))
                return last

            def wide(bank, g, k):
                return pe.matmul(ps[:, bank, :], msg[:, k, :], adjT[:, k, g * GN:(g + 1) * GN],
                                 start=(k == 0), stop=(k + 1 == T))

            def narrow_product(feats, g, bank):
                for k in range(0, T, 2):
                    last = narrow(bank, g, feats, k)
                last.then_inc(acc_done, 1)

            def post(ready, value, lhs, rhs, bank, at=0):
                pe.wait_ge(ready, value)
                for c in range(G):
                    last = pe.matmul(ps[:, bank, at + c * C:at + (c + 1) * C], lhs(c), rhs, start=True, stop=True)
                return last

            def batch(b, is_last):
                def product(i, half):
                    pe.wait_ge(xs_ready, b * T + (i + 1))
                    for o in range(2):
                        g = 2 * half + o
                        last = pe.matmul(ps[o * C:(o + 1) * C, half, :], xs[:, i % 2, :],
                                         work[:, i % 3, g * GN:(g + 1) * GN],
                                         start=(i == 0), stop=(i + 1 == T))
                    if half == 1:
                        last.then_inc(k_used, 1)

                pe.wait_ge(adjT_ready, b * 2 * T + 2 * T)
                for i in range(T):
                    J = T - 1 - i
                    for q in range(NG):
                        if i >= 2 and q % 2 == 0:
                            product(i - 2, q // 2)
                        if i >= 1 and q % 2 == 0:
                            pe.wait_ge(k_ready, b * 2 * T + (2 * (i - 1) + q // 2 + 1))
                        last = pe.matmul(ps[:, 4 + q, :], ustat[:, J * P:(J + 1) * P], umov[:, q * GN:(q + 1) * GN],
                                         start=True, stop=True)
                        if q % 2 == 1:
                            last.then_inc(logits_done, 1)
                for i in (T - 2, T - 1):
                    product(i, 0)
                    product(i, 1)
                for half in range(2):
                    pe.wait_ge(agg_ready, b * AGG_ALL + (half + 1))
                    for c in range(G):
                        last = pe.transpose(ps[:, 2 + half, c * P:(c + 1) * P], agg[:, half, c * P:(c + 1) * P],
                                            ident[:, :])
                    last.then_inc(post_done, 2)

                def first_two(ready, base, feats, tail):
                    for q in range(NG):
                        pe.wait_ge(ready, base + (q + 1))
                        for g in range(2):
                            for k in range(q * G, (q + 1) * G, 2):
                                last = narrow(g, g, feats, k)
                            if q == NG - 1:
                                last.then_inc(acc_done, 1)
                        if q == 0:
                            tail()

                def hidden(g):
                    pe.wait_ge(agg_ready, b * AGG_ALL + (AGG_L1 + g + 1))
                    pe.wait_ge(diag_ready, b * NG + (g + 1))
                    if g >= 2:
                        pe.wait_ge(h_ready, b * 3 * NG + (g - 1))
                    pe.matmul(ps[:, 4 + g % 2, :], w0s[:, :], agg[:, g % 2, :], start=True, stop=False)
                    pe.matmul(ps[:, 4 + g % 2, :], b0b[:, :], diag[:, g % 2, :],
                              start=False, stop=True).then_inc(hidden_done, 1)

                def message(layer, g, w):
                    pe.wait_ge(h_ready, b * 3 * NG + (layer * NG + g + 1))
                    if g >= 2:
                        pe.wait_ge(msg_ready, b * 2 * NG + (layer * NG + g - 1))
                    for c in range(G):
                        t = g * G + c
                        last = pe.matmul(ps[:, 6 + g % 2, c * HID:(c + 1) * HID], hT[:, t * P:(t + 1) * P], w[:, :],
                                         start=True, stop=True)
                    last.then_inc(msg_done, 1)

                first_two(x_ready, b * X_ALL + X_L0, xa, lambda: None)
                narrow_product(xa, 2, 2)
                hidden(0)
                hidden(1)
                narrow_product(xa, 3, 3)
                hidden(2)
                message(0, 0, w1)
                message(0, 1, w1)
                hidden(3)
                message(0, 2, w1)
                message(0, 3, w1)

                for layer in range(2):
                    for q in range(NG):
                        pe.wait_ge(msg_ready, b * 2 * NG + (layer * NG + q + 1))
                        for g in range(2):
                            for k in range(q * G, (q + 1) * G):
                                last = wide(g, g, k)
                            if q == NG - 1:
                                last.then_inc(acc_done, 1)
                    for g in range(2, NG):
                        for k in range(T):
                            last = wide(g, g, k)
                        last.then_inc(acc_done, 1)
                        if layer == 1 and g == 2:
                            for gg in range(2):
                                out_layer(pe, b, gg)
                    if layer == 0:
                        for g in range(NG):
                            message(1, g, w2)
                out_layer(pe, b, 2)

                first_two(x_ready, b * X_ALL + X_L1, xa, lambda: out_layer(pe, b, 3))
                for v in range(2):
                    for u in range(v * G, (v + 1) * G):
                        last = pe.transpose(ps[:, 6 + v, (u % G) * P:(u % G + 1) * P],
                                            xa[:, 2 * u:2 * u + 2, :].rearrange("p t c -> p (t c)"), ident[:, :])
                    last.then_inc(xT_done, 1)

                def post_L2(g):
                    if g >= 2:
                        pe.wait_ge(post_read, b * X_ALL + (X_L2 + g - 1))
                    pe.wait_ge(xT_ready, b * 2 + (g // 2 + 1))
                    for v in range(G // 2):
                        pe.matmul(ps[:, 4 + g % 2, (G + 2 * v) * C:(G + 2 * v + 2) * C],
                                  xT[:, g * G // 2 + v, :], wss[:, :], start=True, stop=True)
                    post(agg_ready, b * AGG_ALL + (AGG_L2 + g + 1), lambda c: agg[:, g % 2, c * P:(c + 1) * P],
                         wns[:, :], 4 + g % 2).then_inc(post_done, 1)

                narrow_product(xa, 2, 2)
                post_L2(0)
                post_L2(1)
                for k in range(0, T, 2):
                    last = narrow(3, 3, xa, k)
                    if k == G:
                        post_L2(2)
                last.then_inc(acc_done, 1)

                def post_L3(g):
                    if g >= 1:
                        pe.wait_ge(post_read, b * X_ALL + (X_L3 + g))
                    post(agg_ready, b * AGG_ALL + (AGG_L3 + g + 1), lambda c: agg[:, g % 2, c * P:(c + 1) * P],
                         wks[:, :], 3).then_inc(post_done, 1)

                for g in range(NG):
                    pe.wait_ge(eye_added, b * NG + (g + 1))
                    for k in range(0, T, 2):
                        if g == 0 and k % G == 0:
                            pe.wait_ge(ys_ready, b * NG + (k // G + 1))
                        last = narrow(g % 3, g, ys, k)
                        if k + 2 == T:
                            last.then_inc(acc_done, 1)
                        if g == 0 and k + 2 == G:
                            post_L2(3)
                        if g >= 1 and k % 4 == 2 and not is_last:
                            flip_row(b + 1, (g - 1) * G + k // 4)
                    if g >= 1:
                        post_L3(g - 1)
                for c in range(G):
                    if not is_last:
                        flip_row(b + 1, (NG - 1) * G + c)
                    if c == 0:
                        post_L3(NG - 1)

            def out_layer(pe, b, g):
                if g >= 2:
                    pe.wait_ge(post_read, b * X_ALL + (X_L1 + g - 1))
                post(h_ready, b * 3 * NG + (2 * NG + g + 1), lambda c: hT[:, (g * G + c) * P:(g * G + c + 1) * P],
                     wout[:, :], 4 + g % 2).then_inc(post_done, 1)

            for I in range(T):
                flip_row(0, I)
            pe.wait_ge(const_loaded, CONSTS * DMA)
            with pe.Fori(0, B - 1) as b:
                batch(b, False)
            batch(B - 1, True)

        @block.scalar
        def _(act):
            for side, dst in enumerate((ustat, umov)):
                for q in range(NG):
                    act.wait_ge(u_flipped, side * NG + q + 1)
                    act.activation(dst[:, q * GN:(q + 1) * GN], ps[:, side * NG + q, 0:GN // 2].bitcast(bf16),
                                   ACT.Copy).then_inc(u_ready, 1)

            def keep_row(b, I):
                for h in range(2):
                    act.wait_ge(row_flipped, b * 2 * T + (2 * I + h + 1))
                    act.activation(adjT[:, h * T // 2:(h + 1) * T // 2, I * P:(I + 1) * P],
                                   ps[:, 4 + 2 * h:6 + 2 * h, :].rearrange("p a (j n) -> p (a j) n", n=P),
                                   ACT.Copy).then_inc(adjT_ready, 1)

            def batch(b, is_last):
                def scale_features(i):
                    J = T - 1 - i
                    act.wait_ge(d_ready, b * T + (i + 1))
                    if i == 0:
                        act.wait_ge(x_loaded, (b + 1) * (NG * DMA))
                    if i >= 2:
                        act.wait_ge(k_used, b * T + (i - 1))
                    act.activation(xs[:, i % 2, :], xa[:, J, :], ACT.Copy, scale=dl0[:, J:J + 1]).then_inc(xs_ready, 1)

                for i in range(T):
                    for h in range(2):
                        if i >= 1 and h == 1:
                            scale_features(i - 1)
                        act.wait_ge(logits_done, b * 2 * T + (2 * i + h + 1))
                        act.activation(ps[:, 4 + 2 * h:6 + 2 * h, :], ps[:, 4 + 2 * h:6 + 2 * h, :],
                                       ACT.Sigmoid).then_inc(sigmoid_done, 1)
                    J = T - 1 - i
                    act.wait_ge(row_loaded[J % SLOTS], K_loaded(b, J))
                    if i == 0:
                        act.wait_ge(dve_added, b * T + 1)
                    act.activation(ps[:, 2:4, :].rearrange("p a n -> p (a n)"), rows[:, J % SLOTS, HALF:N], ACT.Copy,
                                   accum_out=rowpart[:, 1, J:J + 1]).then_inc(half_summed, 1)
                    act.wait_ge(half_summed, b * T + (i + 1))
                scale_features(T - 1)
                act.wait_ge(k_used, b * T + T)
                for half in range(2):
                    act.activation(agg[:, half, :], ps[:, half, :], ACT.Copy).then_inc(agg_ready, 1)

                def keep_agg(acc, g, bank):
                    act.wait_ge(acc_done, b * ACC_ALL + (acc + g + 1))
                    act.activation(agg[:, g % 2, :], ps[:, bank, :], ACT.Copy).then_inc(agg_ready, 1)

                def relu(src, g):
                    act.activation(hT[:, g * GN:(g + 1) * GN], ps[:, src, :], ACT.Relu).then_inc(h_ready, 1)

                keep_agg(ACC_A, 0, 0)
                keep_agg(ACC_A, 1, 1)
                for g in range(2):
                    act.wait_ge(hidden_done, b * NG + (g + 1))
                    relu(4 + g, g)
                keep_agg(ACC_A, 2, 2)
                keep_agg(ACC_A, 3, 3)
                for g in range(2, NG):
                    act.wait_ge(hidden_done, b * NG + (g + 1))
                    relu(4 + g % 2, g)
                for acc in (ACC_B, ACC_C):
                    for g in range(NG):
                        act.wait_ge(acc_done, b * ACC_ALL + (acc + g + 1))
                        relu(g, g)
                keep_agg(ACC_L2, 0, 0)
                keep_agg(ACC_L2, 1, 1)
                for v in range(2):
                    act.wait_ge(xT_done, b * 2 + (v + 1))
                    act.activation(xT[:, v * G:(v + 1) * G, :], ps[:, 6 + v, :].rearrange("p (u n) -> p u n", n=P),
                                   ACT.Copy).then_inc(xT_ready, 1)
                for g in range(2, NG):
                    act.wait_ge(post_done, b * X_ALL + (X_L2 + g - 1))
                    keep_agg(ACC_L2, g, g)
                for g in range(NG):
                    if g >= 2:
                        act.wait_ge(post_done, b * X_ALL + (X_L3 + g - 1))
                    keep_agg(ACC_L3, g, g % 3)
                    if not is_last:
                        for I in range(g * G, (g + 1) * G):
                            keep_row(b + 1, I)

            for I in range(T):
                keep_row(0, I)
            with act.Fori(0, B - 1) as b:
                batch(b, False)
            batch(B - 1, True)

        @block.vector
        def _(dve):
            steps = [0]

            def link(instruction):
                steps[0] += 1
                instruction.then_inc(dve_step, 1)
                dve.wait_ge(dve_step, steps[0])

            def restart():
                dve.sem_clear(dve_step)
                steps[0] = 0

            parts = ((1, 1, 2, 2, 1, 3, 2, 3), (1, 2, 1, 2, 3, 1, 3, 2))
            dve.wait_ge(u_loaded, DMA)
            src = u_nat
            for part in (1, 2, 3):
                for side, nat in enumerate((ustat_nat, umov_nat)):
                    for s in range(8):
                        if parts[side][s] == part:
                            link(dve.tensor_copy(nat[:, :, s, :], src))
                if part < 3:
                    s = parts[0].index(part)
                    link(dve.tensor_sub(u_rest, src, ustat_nat[:, :, s, :]))
                    src = u_rest
            dve.memset(neghalf[:, :], -0.5).then_inc(u_split, 1)
            restart()

            def sum_row(b, I):
                dve.wait_ge(row_loaded[I % SLOTS], T_loaded(b, I))
                dve.reduce_sum(rowpart[:, 0, I:I + 1], rows[:, I % SLOTS, 0:HALF], X).then_inc(row_summed, 2)

            def over(stat):
                return stat.unsqueeze(2).to_broadcast([P, G, C])

            def layer_norm(b, base, g, dst):
                y = yv[g % 2]
                for c in range(G):
                    last = dve.bn_stats(stats[:, c, :], y[:, c, :])
                link(last)
                for c in range(G):
                    last = dve.bn_aggr(moments[:, c, :], stats[:, c, :])
                link(last)
                dve.tensor_scalar(var[:, :], moments[:, :, 1], LN_EPS, None, ALU.add).then_inc(var_ready, 1)
                dve.wait_ge(rstd_ready, b * X_ALL + (base + g + 1))
                for c in range(G):
                    last = dve.tensor_scalar(dst[:, g * G + c, :], y[:, c, :], moments[:, c, 0:1], rstd[:, c:c + 1],
                                             ALU.subtract, ALU.mult)
                last.then_inc(x_ready, 1)
                dve.wait_ge(x_ready, b * X_ALL + (base + g + 1))

            def batch(b, is_last):
                def add_row(i):
                    J = T - 1 - i
                    if i == 0:
                        dve.wait_ge(adjT_ready, b * 2 * T + 2 * T)
                    if i >= 3:
                        dve.wait_ge(k_used, b * T + (i - 2))
                    dve.wait_ge(row_loaded[J % SLOTS], K_loaded(b, J))
                    cut = POOL_COLS[i]
                    dve.tensor_add(work[:, i % 3, cut:N], rows[:, J % SLOTS, cut:N],
                                   adjT[:, J, cut:N]).then_inc(dve_added, 1)

                add_row(0)
                for i in range(T):
                    J = T - 1 - i
                    if i + 1 < T:
                        add_row(i + 1)
                    dve.wait_ge(pool_added, b * T + (i + 1))
                    dve.wait_ge(dve_added, b * T + (i + 1))
                    for h in range(2):
                        dve.wait_ge(sigmoid_done, b * 2 * T + (2 * i + h + 1))
                        part = work[:, i % 3, h * HALF:(h + 1) * HALF]
                        dve.scalar_tensor_tensor(part, ps[:, 4 + 2 * h:6 + 2 * h, :].rearrange("p a n -> p (a n)"),
                                                 0.5, part, ALU.mult, ALU.mult,
                                                 accum_out=kpart[:, J, h:h + 1]).then_inc(k_ready, 1)
                    dve.wait_ge(k_ready, b * 2 * T + (2 * i + 2))
                    dve.tensor_scalar(deg[:, J:J + 1], kpart[:, J, 0:1], kpart[:, J, 1:2], DEG_EPS,
                                      ALU.add, ALU.max).then_inc(deg_ready, 1)
                dve.wait_ge(d_ready, b * T + T)
                dve.wait_ge(const_loaded, CONSTS * DMA)
                dve.wait_ge(half_summed, b * T + T)
                link(dve.tensor_add(rowsum[:, :], rowpart[:, 0, :], rowpart[:, 1, :]))
                link(dve.tensor_scalar(dw[:, :], dl0[:, :], wsc[:, :], None, ALU.mult))

                def result(base, g, bank):
                    dve.wait_ge(post_done, b * X_ALL + (base + g + 1))
                    return ps[:, bank, 0:G * C].rearrange("p (t c) -> p t c", c=C)

                def seen(base, g):
                    dve.wait_ge(post_read, b * X_ALL + (base + g + 1))

                def grp(a, g):
                    return a[:, g * G:(g + 1) * G]

                for g in range(NG):
                    dve.wait_ge(post_done, b * X_ALL + (X_L0 + g + 1))
                    r = ps[:, 2 + g // 2, :].rearrange("p (t o c) -> p t o c", o=2, c=C)[:, :, g % 2, :]
                    dve.tensor_mul(yv[g % 2], r, over(grp(dw, g))).then_inc(post_read, 1)
                    seen(X_L0, g)
                    link(dve.tensor_add(yv[g % 2], yv[g % 2], xa[:, g * G:(g + 1) * G, :]))
                    layer_norm(b, X_L0, g, xa)

                def diag_of(g):
                    if g >= 2:
                        dve.wait_ge(hidden_done, b * NG + (g - 1))
                    dve.tensor_mul(diag[:, g % 2, :].rearrange("p (t n) -> p t n", n=P),
                                   ident[:, :].unsqueeze(1).to_broadcast([P, G, P]),
                                   grp(rowsum, g).unsqueeze(2).to_broadcast([P, G, P])).then_inc(diag_ready, 1)

                def sum_columns(lo, hi):
                    for j in range(lo, hi):
                        last = dve.reduce_sum(colsum[:, j:j + 1], adjT[:, j, :], X)
                    return last

                def keep_message(layer, g, biases):
                    dve.wait_ge(msg_done, b * 2 * NG + (layer * NG + g + 1))
                    dve.tensor_add(msg[:, g * G:(g + 1) * G, :], ps[:, 6 + g % 2, :].rearrange("p (t d) -> p t d", d=HID),
                                   biases[:, :].unsqueeze(1).to_broadcast([P, G, HID])).then_inc(msg_ready, 1)

                diag_of(0)
                diag_of(1)
                sum_columns(0, 5)
                diag_of(2)
                diag_of(3)
                for g in range(NG):
                    keep_message(0, g, b1b)
                sum_columns(5, T - 1)
                link(sum_columns(T - 1, T))
                zero, safe, keep = tiny[:, 0, :], tiny[:, 1, :], tiny[:, 2, :]
                link(dve.tensor_scalar(zero, colsum[:, :], 0.0, None, ALU.is_equal))
                link(dve.tensor_add(safe, colsum[:, :], zero))
                link(dve.reciprocal(safe, safe))
                link(dve.tensor_scalar(keep, zero, -1.0, 1.0, ALU.mult, ALU.add))
                link(dve.tensor_mul(invdeg[:, :], safe, keep))
                link(dve.tensor_scalar(safe, rowsum[:, :], 1.0, None, ALU.add))
                link(dve.tensor_scalar(keep, safe, 0.0, None, ALU.is_gt))
                dve.tensor_scalar(safe, safe, 1e-37, None, ALU.max).then_inc(rowsum_ready, 1)
                dve.wait_ge(dinv_ready, b + 1)
                dve.tensor_mul(dinv[:, :], dinv[:, :], keep).then_inc(dinv_set, 1)
                dve.wait_ge(dinv_set, b + 1)
                dve.wait_ge(acc_done, b * ACC_ALL + (ACC_B + NG))
                for g in range(NG):
                    keep_message(1, g, b2b)
                mask_b = mask[:, b, :] if isinstance(b, int) else \
                    mask[:, bass.ds(b, 1), :].rearrange("p a t -> p (a t)")
                for g in range(NG):
                    r = result(X_L1, g, 4 + g % 2)
                    dve.tensor_mul(yv[g % 2], r, over(grp(mask_b, g))).then_inc(post_read, 1)
                    seen(X_L1, g)
                    if g == 0:
                        dve.wait_ge(x1m_ready, b + 1)
                    link(dve.tensor_add(yv[g % 2], yv[g % 2], x1m[:, g * G:(g + 1) * G, :]))
                    layer_norm(b, X_L1, g, xa)

                for g in range(NG):
                    r = result(X_L2, g, 4 + g % 2)
                    link(dve.tensor_mul(yv[g % 2], r, over(grp(invdeg, g))))
                    dve.tensor_add(yv[g % 2], yv[g % 2], ps[:, 4 + g % 2, G * C:2 * G * C]
                                   .rearrange("p (t c) -> p t c", c=C)).then_inc(post_read, 1)
                    seen(X_L2, g)
                    dve.wait_ge(x2b_ready, b * NG + (g + 1))
                    link(dve.tensor_add(yv[g % 2], yv[g % 2], x2b[:, g * G:(g + 1) * G, :]))
                    layer_norm(b, X_L2, g, xb)

                for g in range(NG):
                    if g >= 1 and not is_last:
                        for I in range((g - 1) * G, g * G):
                            sum_row(b + 1, I)
                    if g == 0:
                        continue
                    post_L3(b, g - 1, result, seen, grp)
                if not is_last:
                    sum_row(b + 1, (NG - 1) * G)
                post_L3(b, NG - 1, result, seen, grp)
                if not is_last:
                    for I in range((NG - 1) * G + 1, T):
                        sum_row(b + 1, I)
                restart()

            def post_L3(b, g, result, seen, grp):
                r = result(X_L3, g, 3)
                dve.tensor_mul(yv[g % 2], r, over(grp(dinv, g))).then_inc(post_read, 1)
                seen(X_L3, g)
                link(dve.scalar_tensor_tensor(yv[g % 2], yv[g % 2], 0.0, xb[:, g * G:(g + 1) * G, :], ALU.max, ALU.add))
                layer_norm(b, X_L3, g, xb)

            for I in range(T):
                sum_row(0, I)
            with dve.Fori(0, B - 1) as b:
                batch(b, False)
            batch(B - 1, True)

        @block.gpsimd
        def _(pool):
            pool.memset(wss[:, :], 0.0).then_inc(wss_cleared, 1)
            pool.memset(ident[:, :], 0.0).then_inc(ident_step, 1)
            pool.wait_ge(ident_step, 1)
            pool.affine_select(out=ident[:, :], in_=ident[:, :], compare_op=ALU.not_equal, fill=1.0, base=0,
                               pattern=[[-1, P]], channel_multiplier=1).then_inc(ident_step, 1)
            pool.wait_ge(ident_step, 2)
            pool.tensor_copy(ident_b, ident[:, :]).then_inc(ident_step, 1)

            def power(dst, base, cols, done):
                pool.tensor_tensor(dst, base, neghalf[:, 0:cols], ALU.pow).then_inc(done, 1)

            def batch(b, is_last):
                def add_row(i):
                    J = T - 1 - i
                    if i >= 3:
                        pool.wait_ge(k_used, b * T + (i - 2))
                    pool.wait_ge(row_loaded[J % SLOTS], K_loaded(b, J))
                    cut = POOL_COLS[i]
                    pool.tensor_add(work[:, i % 3, 0:cut], rows[:, J % SLOTS, 0:cut],
                                    adjT[:, J, 0:cut]).then_inc(pool_added, 1)

                pool.wait_ge(adjT_ready, b * 2 * T + 2 * T)
                add_row(0)
                add_row(1)
                for i in range(T):
                    J = T - 1 - i
                    pool.wait_ge(deg_ready, b * T + (i + 1))
                    power(dl0[:, J:J + 1], deg[:, J:J + 1], 1, d_ready)
                    if i + 2 < T:
                        add_row(i + 2)

                def norm(base, g):
                    pool.wait_ge(var_ready, b * X_ALL + (base + g + 1))
                    power(rstd[:, :], var[:, :], G, rstd_ready)

                def add_bias(g):
                    pool.wait_ge(x_ready, b * X_ALL + (X_L1 + g + 1))
                    pool.tensor_add(x2b[:, g * G:(g + 1) * G, :], xa[:, g * G:(g + 1) * G, :],
                                    biasb[:, :].unsqueeze(1).to_broadcast([P, G, C])).then_inc(x2b_ready, 1)

                for g in range(NG):
                    norm(X_L0, g)
                pool.wait_ge(rowsum_ready, b + 1)
                power(dinv[:, :], tiny[:, 1, :], T, dinv_ready)
                pool.wait_ge(hidden_done, (b + 1) * NG)
                mask_b = mask[:, b, :] if isinstance(b, int) else \
                    mask[:, bass.ds(b, 1), :].rearrange("p a t -> p (a t)")
                pool.wait_ge(x_ready, b * X_ALL + (X_L0 + NG))
                pool.tensor_mul(x1m[:, :, :], boutb[:, :].unsqueeze(1).to_broadcast([P, T, C]),
                                mask_b.unsqueeze(2).to_broadcast([P, T, C])).then_inc(bout_masked, 1)
                pool.wait_ge(bout_masked, b + 1)
                pool.tensor_add(x1m[:, :, :], x1m[:, :, :], xa[:, :, :]).then_inc(x1m_ready, 1)
                for g in range(NG):
                    norm(X_L1, g)
                    if g >= 1:
                        add_bias(g - 1)
                add_bias(NG - 1)
                for g in range(NG):
                    norm(X_L2, g)
                    if g == 0:
                        pool.wait_ge(dinv_set, b + 1)
                    pool.wait_ge(x_ready, b * X_ALL + (X_L2 + g + 1))
                    pool.tensor_mul(ys[:, g * G:(g + 1) * G, :], xb[:, g * G:(g + 1) * G, :],
                                    dinv[:, g * G:(g + 1) * G].unsqueeze(2).to_broadcast([P, G, C]))\
                        .then_inc(ys_ready, 1)
                    pool.wait_ge(acc_done, b * ACC_ALL + (ACC_L2 + g + 1))
                    for k in range(g * G, (g + 1) * G):
                        block_kk = adjT_flat[:, k * (N + P):k * (N + P) + P]
                        last = pool.tensor_add(block_kk, block_kk, ident[:, :])
                    last.then_inc(eye_added, 1)
                for g in range(NG):
                    norm(X_L3, g)

            pool.wait_ge(u_split, 1)
            with pool.Fori(0, B - 1) as b:
                batch(b, False)
            batch(B - 1, True)


CONSTS = 8 + 3 + 4 + 2 + 1


_INS = ['x', 'adj', 'nodemask', 'L0_gnn_U', 'L0_gnn_w_scale', 'L1_gnn_W0', 'L1_gnn_b0', 'L1_gnn_W1', 'L1_gnn_b1',
        'L1_gnn_W2', 'L1_gnn_b2', 'L1_gnn_Wout', 'L1_gnn_bout', 'L2_gnn_W_neighbors', 'L2_gnn_W_self',
        'L2_gnn_bias', 'L3_gnn_kernel']


def kernel(**inputs):
    import concourse.bacc as _bacc
    from concourse.bass_utils import run_bass_kernel_spmd as _run

    nc = _bacc.Bacc("TRN2", target_bir_lowering=False, num_devices=1)
    arrays, args = {}, []
    for name in _INS:
        a = np.ascontiguousarray(inputs[name])
        if a.ndim == 0:
            a = a.reshape(1)
        if name == 'nodemask':
            a = np.ascontiguousarray(a.reshape(a.shape[0], -1, 128).transpose(2, 0, 1))
        arrays[f"in_{name}"] = a
        args.append(nc.dram_tensor(f"in_{name}", a.shape, mybir.dt.from_np(a.dtype), kind="ExternalInput").ap())
    shape = inputs['x'].shape
    args.append(nc.dram_tensor("out_x", shape, mybir.dt.float32, kind="ExternalOutput").ap())
    adjacency_stack_kernel(nc, *args)
    r = _run(nc, [arrays], core_ids=[0])
    return r.results[0]["out_x"]
```

```python
from contextlib import ExitStack

import numpy as np

import concourse.bass as bass
from concourse import mybir


def adjacency_stack_kernel(
    nc: bass.Bass,
    x: bass.AP,
    adj: bass.AP,
    nodemask: bass.AP,
    U: bass.AP,
    w_scale: bass.AP,
    W0: bass.AP,
    b0: bass.AP,
    W1: bass.AP,
    b1: bass.AP,
    W2: bass.AP,
    b2: bass.AP,
    Wout: bass.AP,
    bout: bass.AP,
    W_neighbors: bass.AP,
    W_self: bass.AP,
    bias: bass.AP,
    W_l3: bass.AP,
    out: bass.AP,
):
    fp32 = mybir.dt.float32
    fp32r = mybir.dt.float32r
    bf16 = mybir.dt.bfloat16
    ALU = mybir.AluOpType
    ACT = mybir.ActivationFunctionType
    X = mybir.AxisListType.X

    B, N, C = x.shape
    HID = W1.shape[0]
    R = U.shape[1]
    P = 128
    T = N // P
    G = 4
    NG = T // G
    GN = G * P
    SLOTS = 4
    T_LOADS = T // SLOTS
    K_LOADS = (T - SLOTS) // SLOTS
    LOADS = T_LOADS + K_LOADS
    HI_SLOTS, LO_SLOTS = 4, 3
    TILES = NG * T // 2
    LO_CUT = 368
    MSG_AFTER = [[None, None, None, 2], [TILES // 2 + 2, TILES // 2 + 6, 2, 4]]
    DMA = 16
    EARLY = T - 2
    POOL_COLS = 1344
    ACT_COLS = 9
    OUT_AFTER, SUM_AFTER, VAR_AFTER, POWER_AFTER, NORM_AFTER = (18, 20), (21, 25), (22, 26), (23, 27), (24, 28)
    MASK_AFTER, X1M_AFTER = 10, 14
    L3_POST_AFTER = [(2, 4), (2, 12), (3, 8)]
    FLIP_AFTER = [(2, 0), (2, 2), (2, 4), (2, 6), (2, 10), (2, 14), (3, 0), (3, 2), (3, 6), (3, 8), (3, 10), (3, 14)]
    DEG_EPS = 1e-12
    LN_EPS = 1e-5
    HALF = N // 2
    assert P == 2 * C and HID == P and T == 16 and NG == 4

    with ExitStack() as ctx:
        def sb(name, shape, dt=fp32):
            return ctx.enter_context(nc.sbuf_tensor(name, shape, dt))

        def sem(name):
            return ctx.enter_context(nc.semaphore(name))

        adjT = sb("adjT", [P, T, N])
        rows_at = nc.sbuf_base
        rows = sb("rows", [P, SLOTS, N])
        work_at = nc.sbuf_base
        work = sb("work", [P, 3, N])
        assert work_at == rows_at + SLOTS * N * 4

        adj_hi = nc.alloc_sbuf_tensor_at("adj_hi", [P, HI_SLOTS, 2, GN], fp32r, offset=rows_at)
        adj_lo = nc.alloc_sbuf_tensor_at("adj_lo", [P, LO_SLOTS, 2, GN], fp32r, offset=rows_at + HI_SLOTS * 2 * GN * 4)
        msg_hi = nc.alloc_sbuf_tensor_at("msg_hi", [P, T, HID], fp32r, offset=work_at + N * 4)
        msg_lo = nc.alloc_sbuf_tensor_at("msg_lo", [P, T, HID], fp32r, offset=work_at + 2 * N * 4)
        ustat = sb("ustat", [P, N], bf16)
        umov = sb("umov", [P, N], bf16)
        xa = sb("xa", [P, T, C])
        xb = sb("xb", [P, T, C])
        w0s = sb("w0s", [P, HID])
        w1 = sb("w1", [P, HID])
        w2 = sb("w2", [P, HID])
        wout = sb("wout", [P, C])
        wns = sb("wns", [P, C])
        wss = sb("wss", [P, P])
        wks = sb("wks", [P, C])
        ident = sb("ident", [P, P])
        b0b = sb("b0b", [P, HID])
        b1b = sb("b1b", [P, HID])
        b2b = sb("b2b", [P, HID])
        boutb = sb("boutb", [P, C])
        biasb = sb("biasb", [P, C])
        wsc = sb("wsc", [P, 1])
        mask = sb("mask", [P, B, T])
        neghalf = sb("neghalf", [P, T])
        rowpart = sb("rowpart", [P, 2, T])
        rowsum = sb("rowsum", [P, T])
        colsum = sb("colsum", [P, T])
        kpart = sb("kpart", [P, T, 2])
        deg = sb("deg", [P, T])
        dl0 = sb("dl0", [P, T])
        dw = sb("dw", [P, T])
        invdeg = sb("invdeg", [P, T])
        dinv = sb("dinv", [P, T])
        tiny = sb("tiny", [P, 3, T])
        stats = sb("stats", [P, G, 6])
        moments = sb("moments", [P, G, 2])
        var = sb("var", [P, G])
        rstd = sb("rstd", [P, G])
        xs = sb("xs", [P, 2, C])

        hT = work[:, 0, :]
        ys = work[:, 0, T * C:2 * T * C].rearrange("p (t c) -> p t c", c=C)
        xT = work[:, 1, 0:T * C].rearrange("p (u n) -> p u n", n=P)
        agg = work[:, 2, HALF:HALF + 2 * GN].rearrange("p (s n) -> p s n", n=GN)
        yv = [work[:, 2, i * G * C:(i + 1) * G * C].rearrange("p (t c) -> p t c", c=C) for i in range(2)]
        yv_L1 = [rows[:, SLOTS - 1, HALF + i * G * C:HALF + (i + 1) * G * C].rearrange("p (t c) -> p t c", c=C)
                 for i in range(2)]
        x1m = xb
        x2b = work[:, 0, 0:T * C].rearrange("p (t c) -> p t c", c=C)
        diag = rows[:, SLOTS - 1, HALF:N].rearrange("p (s n) -> p s n", n=GN)
        msg = xb[:, :, :].rearrange("p (s t) c -> p s (t c)", s=2)
        adjT_flat = adjT[:, :, :].rearrange("p j i -> p (j i)")

        u_nat = adjT[:, 0, 0:T * R].rearrange("p (t r) -> p t r", r=R)
        u_rest = adjT[:, 1, 0:T * R].rearrange("p (t r) -> p t r", r=R)
        ustat_nat = adjT[:, 2, 0:HALF].bitcast(bf16).rearrange("p (t s r) -> p t s r", s=8, r=R)
        umov_nat = adjT[:, 3, 0:HALF].bitcast(bf16).rearrange("p (t s r) -> p t s r", s=8, r=R)
        ident_b = adjT[:, 4, 0:P // 2].bitcast(bf16)

        ps = ctx.enter_context(nc.psum_tensor("ps", [P, 8, 512], fp32))

        const_loaded = sem("const_loaded")
        u_loaded = sem("u_loaded")
        wss_cleared = sem("wss_cleared")
        ident_step = sem("ident_step")
        u_split = sem("u_split")
        u_flipped = sem("u_flipped")
        u_ready = sem("u_ready")
        row_loaded = [sem(f"row_loaded{s}") for s in range(SLOTS)]
        x_loaded = sem("x_loaded")
        row_flipped = sem("row_flipped")
        adjT_ready = sem("adjT_ready")
        row_summed = sem("row_summed")
        half_summed = sem("half_summed")
        logits_done = sem("logits_done")
        sigmoid_done = sem("sigmoid_done")
        pool_added = sem("pool_added")
        dve_added = sem("dve_added")
        k_ready = sem("k_ready")
        deg_ready = sem("deg_ready")
        d_ready = sem("d_ready")
        xs_ready = sem("xs_ready")
        k_used = sem("k_used")
        acc_done = sem("acc_done")
        agg_ready = sem("agg_ready")
        hidden_done = sem("hidden_done")
        h_ready = sem("h_ready")
        h_wide_ready = sem("h_wide_ready")
        diag_ready = sem("diag_ready")
        msg_done = sem("msg_done")
        msg_whole = sem("msg_whole")
        msg_hi_ready = sem("msg_hi_ready")
        msg_ready = sem("msg_ready")
        hi_ready = sem("hi_ready")
        lo_dve_ready = sem("lo_dve_ready")
        lo_pool_ready = sem("lo_pool_ready")
        tile_used = sem("tile_used")
        columns_summed = sem("columns_summed")
        post_done = sem("post_done")
        post_read = sem("post_read")
        xT_done = sem("xT_done")
        xT_ready = sem("xT_ready")
        rowsum_ready = sem("rowsum_ready")
        dinv_ready = sem("dinv_ready")
        dinv_set = sem("dinv_set")
        bout_masked = sem("bout_masked")
        x1m_ready = sem("x1m_ready")
        x2b_ready = sem("x2b_ready")
        eye_added = sem("eye_added")
        ys_ready = sem("ys_ready")
        var_ready = sem("var_ready")
        rstd_ready = sem("rstd_ready")
        x_ready = sem("x_ready")
        dve_step = sem("dve_step")
        stored = sem("stored")
        stores_over = sem("stores_over")

        X_L0, X_L1, X_L2, X_L3, X_ALL = 0, NG, 2 * NG, 3 * NG, 4 * NG
        ACC_L1, ACC_L2, ACC_L3, ACC_ALL = [i * NG for i in range(4)]
        AGG_L1, AGG_L2, AGG_L3, AGG_ALL = 2, 2 + NG, 2 + 2 * NG, 2 + 3 * NG

        all_rows = adj.rearrange("b n m -> (b n) m")

        def rows_of(b, J):
            at = b * N + J * P
            return all_rows[at:at + P, :] if isinstance(b, int) else all_rows[bass.ds(at, P), :]

        def nodes_of(a, b):
            v = a[b, :, :] if isinstance(b, int) else a[bass.ds(b, 1), :, :].rearrange("a n c -> (a n) c")
            return v.rearrange("(t p) c -> p t c", p=P)

        def hi_free(b, layer, n):
            if n >= HI_SLOTS:
                return b * 2 * TILES + (layer * TILES + n - HI_SLOTS + 1)
            last = max(m for m in range(TILES) if m % HI_SLOTS == n % HI_SLOTS)
            return b * 2 * TILES + (last + 1) if layer else None

        def lo_free(b, layer, n):
            if n >= LO_SLOTS:
                return b * 2 * TILES + (layer * TILES + n - LO_SLOTS + 1)
            last = max(m for m in range(TILES) if m % LO_SLOTS == n % LO_SLOTS)
            return b * 2 * TILES + (last + 1) if layer else None

        def product_over(b, layer, g):
            last = max(n for n in range(TILES) if place(n)[0] == g)
            return b * 2 * TILES + (layer * TILES + last + 1)

        def place(n):
            pair, q, o, v = n // T, n % T // 4, n % 4 // 2, n % 2
            return 2 * pair + o, 2 * q + v

        def piece(n):
            g, u = place(n)
            return adjT[:, 2 * u:2 * u + 2, g * GN:(g + 1) * GN]

        def behind(table, layer, n):
            return [(m, g) for m in range(2) for g in range(NG) if table[m][g] is not None
                    and (table[m][g] + (m * TILES if g >= 2 or m == 0 else 0)) == layer * TILES + n]

        def later(table, by):
            return [[None if at is None else at + by for at in line] for line in table]

        def T_loaded(b, I):
            return DMA * (b * LOADS + (I // SLOTS + 1))

        def K_loaded(b, J):
            if J >= T - SLOTS:
                return T_loaded(b, J)
            return DMA * (b * LOADS + (T_LOADS + (T - SLOTS - 1 - J) // SLOTS + 1))

        block = ctx.enter_context(nc.Block())

        @block.sync
        def _(sp):
            sp.dma_start(u_nat, U.rearrange("(t p) r -> p t r", p=P)).then_inc(u_loaded, DMA)

            def load_T(b, I):
                if I >= SLOTS:
                    sp.wait_ge(row_flipped, b * 2 * T + 2 * (I - SLOTS + 1))
                    sp.wait_ge(row_summed, b * 2 * T + 2 * (I - SLOTS + 1))
                sp.dma_start(rows[:, I % SLOTS, :], rows_of(b, I)).then_inc(row_loaded[I % SLOTS], DMA)

            def load_K(b, J, src):
                sp.wait_ge(pool_added, b * T + (T - SLOTS - J))
                sp.wait_ge(dve_added, b * T + (T - SLOTS - J))
                sp.wait_ge(half_summed, b * T + (T - SLOTS - J))
                sp.dma_start(rows[:, J % SLOTS, :], src).then_inc(row_loaded[J % SLOTS], DMA)

            def store(b, g):
                sp.wait_ge(x_ready, b * X_ALL + (X_L3 + g + 1))
                sp.dma_start(nodes_of(out, b)[:, g * G:(g + 1) * G, :],
                             xb[:, g * G:(g + 1) * G, :]).then_inc(stored, DMA)

            for I in range(SLOTS):
                load_T(0, I)
            sp.wait_ge(wss_cleared, 1)
            for half in range(2):
                sp.dma_start(wss[half * C:(half + 1) * C, half * C:(half + 1) * C], W_self).then_inc(const_loaded, DMA)
            for dst, src in ((w0s, W0), (wns, W_neighbors), (wks, W_l3)):
                for half in range(2):
                    sp.dma_start(dst[half * C:(half + 1) * C, :], src).then_inc(const_loaded, DMA)
            for dst, src in ((w1, W1), (w2, W2), (wout, Wout)):
                sp.dma_start(dst[:, :], src).then_inc(const_loaded, DMA)
            for dst, src in ((b0b, b0), (b1b, b1), (b2b, b2), (boutb, bout)):
                sp.dma_start(dst[:, :], src.partition_broadcast(P)).then_inc(const_loaded, DMA)
            sp.dma_start(biasb[:, :], bias[0, :].partition_broadcast(P)).then_inc(const_loaded, DMA)
            sp.dma_start(wsc[:, :], w_scale.partition_broadcast(P)).then_inc(const_loaded, DMA)
            sp.dma_start(mask[:, :, :], nodemask).then_inc(const_loaded, DMA)
            for g in range(NG):
                sp.dma_start(xa[:, g * G:(g + 1) * G, :],
                             nodes_of(x, 0)[:, g * G:(g + 1) * G, :]).then_inc(x_loaded, DMA)
            for I in range(SLOTS, T):
                load_T(0, I)

            def batch(b, last, after=B):
                for J in range(T - SLOTS - 1, -1, -1):
                    at = after * N - (N - J * P)
                    load_K(b, J, all_rows[at:at + P, :] if last else all_rows[bass.ds(at, P), :])
                if not last:
                    sp.wait_ge(tile_used, b * 2 * TILES + 2 * TILES)
                    for I in (1, 2, 0):
                        load_T(b + 1, I)
                    sp.wait_ge(x_ready, b * X_ALL + X_L2)
                    load_T(b + 1, SLOTS - 1)
                    sp.wait_ge(x_ready, b * X_ALL + X_L3)
                    for g in (1, 2, 3, 0):
                        sp.dma_start(xa[:, g * G:(g + 1) * G, :],
                                     nodes_of(x, b + 1)[:, g * G:(g + 1) * G, :]).then_inc(x_loaded, DMA)
                if not last:
                    for I in range(SLOTS, T):
                        load_T(b + 1, I)
                for g in range(NG):
                    store(b, g)
                sp.wait_ge(stored, (b + 1) * NG * DMA)
                sp.sem_inc(stores_over, 1)

            with sp.Fori(1, B) as after:
                batch(after - 1, False, after)
            batch(B - 1, True)

        @block.tensor
        def _(pe):
            pe.wait_ge(u_split, 1)
            pe.wait_ge(ident_step, 3)
            for side, nat in enumerate((ustat_nat, umov_nat)):
                for q in range(NG):
                    dst = ps[:, side * NG + q, 0:GN // 2].bitcast(bf16)
                    for c in range(G):
                        last = pe.transpose(dst[:, c * P:(c + 1) * P],
                                            nat[:, q * G + c, :, :].rearrange("p s r -> p (s r)"), ident_b)
                    last.then_inc(u_flipped, 1)
            pe.wait_ge(u_ready, 2 * NG)

            def flip_row(b, I):
                pe.wait_ge(row_loaded[I % SLOTS], T_loaded(b, I))
                for h in range(2):
                    if I >= 1:
                        pe.wait_ge(adjT_ready, b * 2 * T + (2 * (I - 1) + h + 1))
                    for j in range(T // 2):
                        last = pe.transpose(ps[:, 4 + 2 * h + j // G, (j % G) * P:(j % G + 1) * P],
                                            rows[:, I % SLOTS, (h * T // 2 + j) * P:(h * T // 2 + j + 1) * P],
                                            ident[:, :])
                    last.then_inc(row_flipped, 1)

            def narrow(bank, g, feats, k):
                for o in range(2):
                    last = pe.matmul(ps[o * C:(o + 1) * C, bank, :], feats[:, k + o, :],
                                     adjT[:, k + o, g * GN:(g + 1) * GN], start=(k == 0), stop=(k + 2 == T))
                return last

            def wide_piece(b, layer, n):
                (g, u), h, l = place(n), n % HI_SLOTS, n % LO_SLOTS
                first = layer * TILES + n + 1
                pe.wait_ge(hi_ready, b * 2 * TILES + first)
                pe.wait_ge(lo_dve_ready, b * 2 * TILES + first)
                pe.wait_ge(lo_pool_ready, b * 2 * TILES + first)
                for o in range(2):
                    k = 2 * u + o
                    pe.matmul(ps[:, g, :], msg_hi[:, k, :], adj_hi[:, h, o, :], start=(k == 0), stop=False)
                    pe.matmul(ps[:, g, :], msg_hi[:, k, :], adj_lo[:, l, o, :], start=False, stop=False)
                    last = pe.matmul(ps[:, g, :], msg_lo[:, k, :], adj_hi[:, h, o, :], start=False, stop=(k + 1 == T))
                last.then_inc(tile_used, 1)

            def narrow_product(feats, g, bank):
                for k in range(0, T, 2):
                    last = narrow(bank, g, feats, k)
                last.then_inc(acc_done, 1)

            def post(ready, value, lhs, rhs, bank, at=0):
                pe.wait_ge(ready, value)
                for c in range(G):
                    last = pe.matmul(ps[:, bank, at + c * C:at + (c + 1) * C], lhs(c), rhs, start=True, stop=True)
                return last

            def batch(b, is_last):
                def product(i, half):
                    pe.wait_ge(xs_ready, b * T + (i + 1))
                    for o in range(2):
                        g = 2 * half + o
                        last = pe.matmul(ps[o * C:(o + 1) * C, half, :], xs[:, i % 2, :],
                                         work[:, i % 3, g * GN:(g + 1) * GN],
                                         start=(i == 0), stop=(i + 1 == T))
                    if half == 1:
                        last.then_inc(k_used, 1)

                for i in range(T):
                    J = T - 1 - i
                    for q in range(NG):
                        if i >= 2 and q % 2 == 0:
                            product(i - 2, q // 2)
                        if i == 0 and q % 2 == 0:
                            pe.wait_ge(adjT_ready, b * 2 * T + (2 * T - 1 + q // 2))
                        if i >= 1 and q % 2 == 0:
                            pe.wait_ge(k_ready, b * 2 * T + (2 * (i - 1) + q // 2 + 1))
                        last = pe.matmul(ps[:, 4 + q, :], ustat[:, J * P:(J + 1) * P], umov[:, q * GN:(q + 1) * GN],
                                         start=True, stop=True)
                        if q % 2 == 1:
                            last.then_inc(logits_done, 1)
                for i in (T - 2, T - 1):
                    product(i, 0)
                    product(i, 1)
                for half in range(2):
                    pe.wait_ge(agg_ready, b * AGG_ALL + (half + 1))
                    for c in range(G):
                        last = pe.transpose(ps[:, 2 + half, c * P:(c + 1) * P], agg[:, half, c * P:(c + 1) * P],
                                            ident[:, :])
                    last.then_inc(post_done, 2)

                def first_two(ready, base, feats, tail):
                    for q in range(NG):
                        pe.wait_ge(ready, base + (q + 1))
                        for g in range(2):
                            for k in range(q * G, (q + 1) * G, 2):
                                last = narrow(g, g, feats, k)
                            if q == NG - 1:
                                last.then_inc(acc_done, 1)
                            if q == 0 and g == 0:
                                tail()

                def hidden(g):
                    pe.wait_ge(agg_ready, b * AGG_ALL + (AGG_L1 + g + 1))
                    pe.wait_ge(diag_ready, b * NG + (g + 1))
                    if g >= 2:
                        pe.wait_ge(h_ready, b * NG + (g - 1))
                    pe.matmul(ps[:, 4 + g % 2, :], w0s[:, :], agg[:, g % 2, :], start=True, stop=False)
                    pe.matmul(ps[:, 4 + g % 2, :], b0b[:, :], diag[:, g % 2, :],
                              start=False, stop=True).then_inc(hidden_done, 1)

                def message(layer, g, w):
                    if layer == 0:
                        pe.wait_ge(h_ready, b * NG + (g + 1))
                    else:
                        pe.wait_ge(h_wide_ready, b * 2 * NG + (g + 1))
                    if g >= 2:
                        pe.wait_ge(msg_whole, b * 2 * NG + (layer * NG + g - 1))
                    for c in range(G):
                        t = g * G + c
                        last = pe.matmul(ps[:, 6 + g % 2, c * HID:(c + 1) * HID], hT[:, t * P:(t + 1) * P], w[:, :],
                                         start=True, stop=True)
                    last.then_inc(msg_done, 1)

                first_two(x_ready, b * X_ALL + X_L0, xa, lambda: None)
                narrow_product(xa, 2, 2)
                hidden(0)
                hidden(1)
                for k in range(0, T, 2):
                    last = narrow(3, 3, xa, k)
                    if k + 2 == T // 2:
                        hidden(2)
                        message(0, 0, w1)
                        message(0, 1, w1)
                last.then_inc(acc_done, 1)
                message(0, 2, w1)

                for layer in range(2):
                    for n in range(TILES):
                        if n < T and n % 4 == 0:
                            pe.wait_ge(msg_ready, b * 2 * NG + (layer * NG + n // 4 + 1))
                        wide_piece(b, layer, n)
                        if layer == 0 and n == 0:
                            hidden(3)
                        for m, g in behind(MSG_AFTER, layer, n):
                            message(m, g, (w1, w2)[m])
                        if layer == 1 and n in OUT_AFTER:
                            out_layer(pe, b, OUT_AFTER.index(n))
                out_layer(pe, b, 2)

                first_two(x_ready, b * X_ALL + X_L1, xa, lambda: out_layer(pe, b, 3))
                for v in range(2):
                    for u in range(v * G, (v + 1) * G):
                        last = pe.transpose(ps[:, 6 + v, (u % G) * P:(u % G + 1) * P],
                                            xa[:, 2 * u:2 * u + 2, :].rearrange("p t c -> p (t c)"), ident[:, :])
                    last.then_inc(xT_done, 1)

                def post_L2(g):
                    if g >= 2:
                        pe.wait_ge(post_read, b * X_ALL + (X_L2 + g - 1))
                    pe.wait_ge(xT_ready, b * 2 + (g // 2 + 1))
                    for v in range(G // 2):
                        pe.matmul(ps[:, 4 + g % 2, (G + 2 * v) * C:(G + 2 * v + 2) * C],
                                  xT[:, g * G // 2 + v, :], wss[:, :], start=True, stop=True)
                    post(agg_ready, b * AGG_ALL + (AGG_L2 + g + 1), lambda c: agg[:, g % 2, c * P:(c + 1) * P],
                         wns[:, :], 4 + g % 2).then_inc(post_done, 1)

                narrow_product(xa, 2, 2)
                post_L2(0)
                post_L2(1)
                for k in range(0, T, 2):
                    last = narrow(3, 3, xa, k)
                    if k == G:
                        post_L2(2)
                last.then_inc(acc_done, 1)

                def post_L3(g):
                    if g >= 1:
                        pe.wait_ge(post_read, b * X_ALL + (X_L3 + g))
                    post(agg_ready, b * AGG_ALL + (AGG_L3 + g + 1), lambda c: agg[:, g % 2, c * P:(c + 1) * P],
                         wks[:, :], 3).then_inc(post_done, 1)

                pe.wait_ge(eye_added, b * NG + 2)
                first_two(ys_ready, b * NG, ys, lambda: post_L2(3))
                for g in range(2, NG):
                    pe.wait_ge(eye_added, b * NG + (g + 1))
                    for k in range(0, T, 2):
                        last = narrow(g % 3, g, ys, k)
                        if k + 2 == T:
                            last.then_inc(acc_done, 1)
                        if (g, k) in FLIP_AFTER and not is_last:
                            flip_row(b + 1, FLIP_AFTER.index((g, k)))
                        if (g, k) in L3_POST_AFTER:
                            post_L3(L3_POST_AFTER.index((g, k)))
                for I in range(len(FLIP_AFTER), T):
                    if not is_last:
                        flip_row(b + 1, I)
                    if I == len(FLIP_AFTER):
                        post_L3(NG - 1)

            def out_layer(pe, b, g):
                if g >= 2:
                    pe.wait_ge(post_read, b * X_ALL + (X_L1 + g - 1))
                post(h_wide_ready, b * 2 * NG + (NG + g + 1), lambda c: hT[:, (g * G + c) * P:(g * G + c + 1) * P],
                     wout[:, :], 4 + g % 2).then_inc(post_done, 1)

            for I in range(T):
                flip_row(0, I)
            pe.wait_ge(const_loaded, CONSTS * DMA)
            with pe.Fori(0, B - 1) as b:
                batch(b, False)
            batch(B - 1, True)

        @block.scalar
        def _(act):
            for side, dst in enumerate((ustat, umov)):
                for q in range(NG):
                    act.wait_ge(u_flipped, side * NG + q + 1)
                    act.activation(dst[:, q * GN:(q + 1) * GN], ps[:, side * NG + q, 0:GN // 2].bitcast(bf16),
                                   ACT.Copy).then_inc(u_ready, 1)

            def keep_row(b, I):
                for h in range(2):
                    act.wait_ge(row_flipped, b * 2 * T + (2 * I + h + 1))
                    act.activation(adjT[:, h * T // 2:(h + 1) * T // 2, I * P:(I + 1) * P],
                                   ps[:, 4 + 2 * h:6 + 2 * h, :].rearrange("p a (j n) -> p (a j) n", n=P),
                                   ACT.Copy).then_inc(adjT_ready, 1)

            def batch(b, is_last):
                def scale_features(i):
                    J = T - 1 - i
                    act.wait_ge(d_ready, b * T + (i + 1))
                    if i == 0:
                        act.wait_ge(x_loaded, (b + 1) * (NG * DMA))
                    if i >= 2:
                        act.wait_ge(k_used, b * T + (i - 1))
                    act.activation(xs[:, i % 2, :], xa[:, J, :], ACT.Copy, scale=dl0[:, J:J + 1]).then_inc(xs_ready, 1)

                for i in range(T):
                    for h in range(2):
                        if i >= 1 and h == 1:
                            scale_features(i - 1)
                        act.wait_ge(logits_done, b * 2 * T + (2 * i + h + 1))
                        act.activation(ps[:, 4 + 2 * h:6 + 2 * h, :], ps[:, 4 + 2 * h:6 + 2 * h, :],
                                       ACT.Sigmoid).then_inc(sigmoid_done, 1)
                    J = T - 1 - i
                    act.wait_ge(row_loaded[J % SLOTS], K_loaded(b, J))
                    if i == 0:
                        act.wait_ge(dve_added, b * T + 1)
                    act.activation(ps[:, 2:4, :].rearrange("p a n -> p (a n)"), rows[:, J % SLOTS, HALF:N], ACT.Copy,
                                   accum_out=rowpart[:, 1, J:J + 1]).then_inc(half_summed, 1)
                    act.wait_ge(half_summed, b * T + (i + 1))
                scale_features(T - 1)
                act.wait_ge(k_used, b * T + T)
                for half in range(2):
                    act.activation(agg[:, half, :], ps[:, half, :], ACT.Copy).then_inc(agg_ready, 1)

                def keep_agg(acc, g, bank):
                    act.wait_ge(acc_done, b * ACC_ALL + (acc + g + 1))
                    act.activation(agg[:, g % 2, :], ps[:, bank, :], ACT.Copy).then_inc(agg_ready, 1)

                def relu(src, g):
                    act.activation(hT[:, g * GN:(g + 1) * GN], ps[:, src, :], ACT.Relu).then_inc(h_ready, 1)

                def sum_columns(lo, hi):
                    for j in range(lo, hi):
                        act.activation(adj_hi[:, 0:2, :, :].rearrange("p s a n -> p (s a n)"), adjT[:, j, :], ACT.Copy,
                                       accum_out=colsum[:, j:j + 1]).then_inc(columns_summed, 1)
                        act.wait_ge(columns_summed, b * ACT_COLS + (j + 1))

                sum_columns(0, 6)
                keep_agg(ACC_L1, 0, 0)
                keep_agg(ACC_L1, 1, 1)
                sum_columns(6, ACT_COLS)
                for g in range(2):
                    act.wait_ge(hidden_done, b * NG + (g + 1))
                    relu(4 + g, g)
                keep_agg(ACC_L1, 2, 2)

                def round_adj(layer, n):
                    free = hi_free(b, layer, n)
                    if free is not None:
                        act.wait_ge(tile_used, free)
                    act.activation(adj_hi[:, n % HI_SLOTS, :, :], piece(n), ACT.Copy).then_inc(hi_ready, 1)

                def round_msg(layer, g):
                    if layer == 1:
                        act.wait_ge(tile_used, b * 2 * TILES + (T + 4 * g + 4))
                    act.wait_ge(msg_whole, b * 2 * NG + (layer * NG + g + 1))
                    act.activation(msg_hi[:, g * G:(g + 1) * G, :].rearrange("p t d -> p (t d)"), msg[:, g % 2, :],
                                   ACT.Copy).then_inc(msg_hi_ready, 1)

                for n in range(2):
                    round_adj(0, n)
                act.wait_ge(hidden_done, b * NG + 3)
                relu(4, 2)
                round_msg(0, 0)
                round_msg(0, 1)
                round_adj(0, 2)
                round_adj(0, 3)
                keep_agg(ACC_L1, 3, 3)
                for layer in range(2):
                    for n in range(HI_SLOTS if layer == 0 else 0, TILES):
                        round_adj(layer, n)
                        if layer == 0 and n == HI_SLOTS:
                            round_msg(0, 2)
                            act.wait_ge(hidden_done, b * NG + NG)
                            relu(5, 3)
                        for m, g in behind(later(MSG_AFTER, 5), layer, n):
                            round_msg(m, g)
                keep_agg(ACC_L2, 0, 0)
                keep_agg(ACC_L2, 1, 1)
                for v in range(2):
                    act.wait_ge(xT_done, b * 2 + (v + 1))
                    act.activation(xT[:, v * G:(v + 1) * G, :], ps[:, 6 + v, :].rearrange("p (u n) -> p u n", n=P),
                                   ACT.Copy).then_inc(xT_ready, 1)
                for g in range(2, NG):
                    act.wait_ge(post_done, b * X_ALL + (X_L2 + g - 1))
                    keep_agg(ACC_L2, g, g)
                for g in range(NG):
                    if g >= 2:
                        act.wait_ge(post_done, b * X_ALL + (X_L3 + g - 1))
                    keep_agg(ACC_L3, g, g % 3)
                    if not is_last:
                        for I in ((), range(0, 5), range(5, 11), range(11, T))[g]:
                            keep_row(b + 1, I)

            for I in range(T):
                keep_row(0, I)
            with act.Fori(0, B - 1) as b:
                batch(b, False)
            batch(B - 1, True)

        @block.vector
        def _(dve):
            steps = [0]

            def link(instruction):
                steps[0] += 1
                instruction.then_inc(dve_step, 1)
                dve.wait_ge(dve_step, steps[0])

            def restart():
                dve.sem_clear(dve_step)
                steps[0] = 0

            parts = ((1, 1, 2, 2, 1, 3, 2, 3), (1, 2, 1, 2, 3, 1, 3, 2))
            dve.wait_ge(u_loaded, DMA)
            src = u_nat
            for part in (1, 2, 3):
                for side, nat in enumerate((ustat_nat, umov_nat)):
                    for s in range(8):
                        if parts[side][s] == part:
                            link(dve.tensor_copy(nat[:, :, s, :], src))
                if part < 3:
                    s = parts[0].index(part)
                    link(dve.tensor_sub(u_rest, src, ustat_nat[:, :, s, :]))
                    src = u_rest
            dve.memset(neghalf[:, :], -0.5).then_inc(u_split, 1)
            restart()

            def sum_row(b, I):
                dve.wait_ge(row_loaded[I % SLOTS], T_loaded(b, I))
                dve.reduce_sum(rowpart[:, 0, I:I + 1], rows[:, I % SLOTS, 0:HALF], X).then_inc(row_summed, 2)

            def over(stat):
                return stat.unsqueeze(2).to_broadcast([P, G, C])

            def layer_norm(b, base, g, dst, yv=yv):
                variance(yv[g % 2])
                normalise(b, base, g, dst, yv)

            def variance(y):
                for c in range(G):
                    last = dve.bn_stats(stats[:, c, :], y[:, c, :])
                link(last)
                for c in range(G):
                    last = dve.bn_aggr(moments[:, c, :], stats[:, c, :])
                link(last)
                dve.tensor_scalar(var[:, :], moments[:, :, 1], LN_EPS, None, ALU.add).then_inc(var_ready, 1)

            def normalise(b, base, g, dst, yv):
                y = yv[g % 2]
                dve.wait_ge(rstd_ready, b * X_ALL + (base + g + 1))
                for c in range(G):
                    last = dve.tensor_scalar(dst[:, g * G + c, :], y[:, c, :], moments[:, c, 0:1], rstd[:, c:c + 1],
                                             ALU.subtract, ALU.mult)
                last.then_inc(x_ready, 1)
                dve.wait_ge(x_ready, b * X_ALL + (base + g + 1))

            def batch(b, is_last):
                def add_row(i):
                    J = T - 1 - i
                    if i >= 3:
                        dve.wait_ge(k_used, b * T + (i - 2))
                    dve.wait_ge(row_loaded[J % SLOTS], K_loaded(b, J))
                    cut = POOL_COLS
                    if i == 0:
                        dve.wait_ge(adjT_ready, b * 2 * T + EARLY * 2)
                        dve.tensor_add(work[:, 0, cut:EARLY * P], rows[:, J % SLOTS, cut:EARLY * P],
                                       adjT[:, J, cut:EARLY * P])
                        cut = EARLY * P
                        dve.wait_ge(adjT_ready, b * 2 * T + 2 * T)
                    dve.tensor_add(work[:, i % 3, cut:N], rows[:, J % SLOTS, cut:N],
                                   adjT[:, J, cut:N]).then_inc(dve_added, 1)

                add_row(0)
                for i in range(T):
                    J = T - 1 - i
                    dve.wait_ge(pool_added, b * T + (i + 1))
                    dve.wait_ge(dve_added, b * T + (i + 1))
                    for h in range(2):
                        if h == 1 and i + 1 < T:
                            add_row(i + 1)
                        dve.wait_ge(sigmoid_done, b * 2 * T + (2 * i + h + 1))
                        part = work[:, i % 3, h * HALF:(h + 1) * HALF]
                        dve.scalar_tensor_tensor(part, ps[:, 4 + 2 * h:6 + 2 * h, :].rearrange("p a n -> p (a n)"),
                                                 0.5, part, ALU.mult, ALU.mult,
                                                 accum_out=kpart[:, J, h:h + 1]).then_inc(k_ready, 1)
                    dve.wait_ge(k_ready, b * 2 * T + (2 * i + 2))
                    dve.tensor_scalar(deg[:, J:J + 1], kpart[:, J, 0:1], kpart[:, J, 1:2], DEG_EPS,
                                      ALU.add, ALU.max).then_inc(deg_ready, 1)
                dve.wait_ge(d_ready, b * T + T)
                dve.wait_ge(const_loaded, CONSTS * DMA)
                dve.wait_ge(half_summed, b * T + T)
                link(dve.tensor_add(rowsum[:, :], rowpart[:, 0, :], rowpart[:, 1, :]))
                link(dve.tensor_scalar(dw[:, :], dl0[:, :], wsc[:, :], None, ALU.mult))

                def result(base, g, bank):
                    dve.wait_ge(post_done, b * X_ALL + (base + g + 1))
                    return ps[:, bank, 0:G * C].rearrange("p (t c) -> p t c", c=C)

                def seen(base, g):
                    dve.wait_ge(post_read, b * X_ALL + (base + g + 1))

                def grp(a, g):
                    return a[:, g * G:(g + 1) * G]

                for g in range(NG):
                    dve.wait_ge(post_done, b * X_ALL + (X_L0 + g + 1))
                    r = ps[:, 2 + g // 2, :].rearrange("p (t o c) -> p t o c", o=2, c=C)[:, :, g % 2, :]
                    dve.tensor_mul(yv[g % 2], r, over(grp(dw, g))).then_inc(post_read, 1)
                    seen(X_L0, g)
                    link(dve.tensor_add(yv[g % 2], yv[g % 2], xa[:, g * G:(g + 1) * G, :]))
                    layer_norm(b, X_L0, g, xa)

                def diag_of(g):
                    if g >= 2:
                        dve.wait_ge(hidden_done, b * NG + (g - 1))
                    dve.tensor_mul(diag[:, g % 2, :].rearrange("p (t n) -> p t n", n=P),
                                   ident[:, :].unsqueeze(1).to_broadcast([P, G, P]),
                                   grp(rowsum, g).unsqueeze(2).to_broadcast([P, G, P])).then_inc(diag_ready, 1)

                def sum_columns(lo, hi):
                    for j in range(lo, hi):
                        last = dve.reduce_sum(colsum[:, j:j + 1], adjT[:, j, :], X)
                    return last

                def keep_message(layer, g, biases):
                    dve.wait_ge(msg_done, b * 2 * NG + (layer * NG + g + 1))
                    if layer * NG + g >= 2:
                        dve.wait_ge(msg_ready, b * 2 * NG + (layer * NG + g - 1))
                    dve.tensor_add(msg[:, g % 2, :].rearrange("p (t d) -> p t d", d=HID),
                                   ps[:, 6 + g % 2, :].rearrange("p (t d) -> p t d", d=HID),
                                   biases[:, :].unsqueeze(1).to_broadcast([P, G, HID])).then_inc(msg_whole, 1)

                def rest_of_adj(layer, n):
                    dve.wait_ge(hi_ready, b * 2 * TILES + (layer * TILES + n + 1))
                    free = lo_free(b, layer, n)
                    if free is not None:
                        dve.wait_ge(tile_used, free)
                    dve.tensor_sub(adj_lo[:, n % LO_SLOTS, :, 0:LO_CUT], piece(n)[:, :, 0:LO_CUT],
                                   adj_hi[:, n % HI_SLOTS, :, 0:LO_CUT].bitcast(fp32)).then_inc(lo_dve_ready, 1)

                diag_of(0)
                diag_of(1)
                sum_columns(ACT_COLS, T - 3)
                diag_of(2)
                diag_of(3)
                link(sum_columns(T - 3, T))
                zero, safe, keep = tiny[:, 0, :], tiny[:, 1, :], tiny[:, 2, :]

                def invert_columns():
                    dve.wait_ge(columns_summed, (b + 1) * ACT_COLS)
                    link(dve.tensor_scalar(zero, colsum[:, :], 0.0, None, ALU.is_equal))
                    link(dve.tensor_add(safe, colsum[:, :], zero))
                    link(dve.reciprocal(safe, safe))
                    link(dve.tensor_scalar(keep, zero, -1.0, 1.0, ALU.mult, ALU.add))
                    link(dve.tensor_mul(invdeg[:, :], safe, keep))

                def guard_rows():
                    link(dve.tensor_scalar(safe, rowsum[:, :], 1.0, None, ALU.add))
                    link(dve.tensor_scalar(keep, safe, 0.0, None, ALU.is_gt))
                    dve.tensor_scalar(safe, safe, 1e-37, None, ALU.max).then_inc(rowsum_ready, 1)

                rest_of_adj(0, 0)
                rest_of_adj(0, 1)
                keep_message(0, 0, b1b)
                keep_message(0, 1, b1b)
                rest_of_adj(0, 2)
                keep_message(0, 2, b1b)
                def relu_wide(layer, g):
                    dve.wait_ge(tile_used, product_over(b, layer, g))
                    dve.tensor_scalar(hT[:, g * GN:(g + 1) * GN], ps[:, g, :], 0.0, None, ALU.max)\
                        .then_inc(h_wide_ready, 1)

                for layer in range(2):
                    for n in range(LO_SLOTS if layer == 0 else 0, TILES):
                        rest_of_adj(layer, n)
                        if layer == 1 and n in (0, 2):
                            relu_wide(0, 2 + n // 2)
                        if n in (T, T + 2):
                            relu_wide(layer, (n - T) // 2)
                        if layer == 0 and n == 9:
                            invert_columns()
                        if layer == 0 and n == 13:
                            guard_rows()
                        for m, g in behind(later(MSG_AFTER, 3), layer, n):
                            keep_message(m, g, (b1b, b2b)[m])
                        if layer == 1 and n in SUM_AFTER:
                            sum_L1(b, SUM_AFTER.index(n), result, seen, grp)
                        if layer == 1 and n in VAR_AFTER:
                            variance(yv_L1[VAR_AFTER.index(n)])
                        if layer == 1 and n in NORM_AFTER:
                            normalise(b, X_L1, NORM_AFTER.index(n), xa, yv_L1)
                relu_wide(1, 2)
                relu_wide(1, 3)
                post_L1(b, 2, result, seen, grp)
                post_L1(b, 3, result, seen, grp)

                dve.wait_ge(dinv_ready, b + 1)
                dve.tensor_mul(dinv[:, :], dinv[:, :], keep).then_inc(dinv_set, 1)
                for g in range(NG):
                    r = result(X_L2, g, 4 + g % 2)
                    link(dve.tensor_mul(yv[g % 2], r, over(grp(invdeg, g))))
                    dve.tensor_add(yv[g % 2], yv[g % 2], ps[:, 4 + g % 2, G * C:2 * G * C]
                                   .rearrange("p (t c) -> p t c", c=C)).then_inc(post_read, 1)
                    seen(X_L2, g)
                    dve.wait_ge(x2b_ready, b * NG + (g + 1))
                    link(dve.tensor_add(yv[g % 2], yv[g % 2], x2b[:, g * G:(g + 1) * G, :]))
                    layer_norm(b, X_L2, g, xb)

                for before, g, between in ((range(0, 4), 0, (4,)), ((), 1, (5,)), ((6, 7, 8), 2, (9,)),
                                           ((10, 11), 3, (12,)), ((13, 14, 15), None, ())):
                    if not is_last:
                        for I in before:
                            sum_row(b + 1, I)
                    if g is not None:
                        sum_L3(b, g, result, seen, grp)
                        variance(yv[g % 2])
                        if not is_last:
                            for I in between:
                                sum_row(b + 1, I)
                        normalise(b, X_L3, g, xb, yv)
                restart()

            def sum_L1(b, g, result, seen, grp):
                mask_b = mask[:, b, :] if isinstance(b, int) else \
                    mask[:, bass.ds(b, 1), :].rearrange("p a t -> p (a t)")
                r = result(X_L1, g, 4 + g % 2)
                dve.tensor_mul(yv_L1[g % 2], r, over(grp(mask_b, g))).then_inc(post_read, 1)
                seen(X_L1, g)
                dve.wait_ge(x1m_ready, b * NG + (g + 1))
                link(dve.tensor_add(yv_L1[g % 2], yv_L1[g % 2], x1m[:, g * G:(g + 1) * G, :]))

            def post_L1(b, g, result, seen, grp):
                sum_L1(b, g, result, seen, grp)
                layer_norm(b, X_L1, g, xa, yv_L1)

            def sum_L3(b, g, result, seen, grp):
                r = result(X_L3, g, 3)
                dve.tensor_mul(yv[g % 2], r, over(grp(dinv, g))).then_inc(post_read, 1)
                seen(X_L3, g)
                link(dve.scalar_tensor_tensor(yv[g % 2], yv[g % 2], 0.0, xb[:, g * G:(g + 1) * G, :], ALU.max, ALU.add))

            for I in range(T):
                sum_row(0, I)
            with dve.Fori(0, B - 1) as b:
                batch(b, False)
            batch(B - 1, True)

        @block.gpsimd
        def _(pool):
            pool.memset(wss[:, :], 0.0).then_inc(wss_cleared, 1)
            pool.memset(ident[:, :], 0.0).then_inc(ident_step, 1)
            pool.wait_ge(ident_step, 1)
            pool.affine_select(out=ident[:, :], in_=ident[:, :], compare_op=ALU.not_equal, fill=1.0, base=0,
                               pattern=[[-1, P]], channel_multiplier=1).then_inc(ident_step, 1)
            pool.wait_ge(ident_step, 2)
            pool.tensor_copy(ident_b, ident[:, :]).then_inc(ident_step, 1)

            def power(dst, base, cols, done):
                pool.tensor_tensor(dst, base, neghalf[:, 0:cols], ALU.pow).then_inc(done, 1)

            def batch(b, is_last):
                def add_row(i):
                    J = T - 1 - i
                    if i >= 3:
                        pool.wait_ge(k_used, b * T + (i - 2))
                    pool.wait_ge(row_loaded[J % SLOTS], K_loaded(b, J))
                    cut = POOL_COLS
                    pool.tensor_add(work[:, i % 3, 0:cut], rows[:, J % SLOTS, 0:cut],
                                    adjT[:, J, 0:cut]).then_inc(pool_added, 1)

                pool.wait_ge(adjT_ready, b * 2 * T + EARLY * 2)
                add_row(0)
                pool.wait_ge(adjT_ready, b * 2 * T + 2 * T)
                add_row(1)
                for i in range(T):
                    J = T - 1 - i
                    pool.wait_ge(deg_ready, b * T + (i + 1))
                    power(dl0[:, J:J + 1], deg[:, J:J + 1], 1, d_ready)
                    if i + 2 < T:
                        add_row(i + 2)

                def norm(base, g):
                    pool.wait_ge(var_ready, b * X_ALL + (base + g + 1))
                    power(rstd[:, :], var[:, :], G, rstd_ready)

                def add_bias(g):
                    pool.wait_ge(x_ready, b * X_ALL + (X_L1 + g + 1))
                    pool.tensor_add(x2b[:, g * G:(g + 1) * G, :], xa[:, g * G:(g + 1) * G, :],
                                    biasb[:, :].unsqueeze(1).to_broadcast([P, G, C])).then_inc(x2b_ready, 1)

                for g in range(NG):
                    norm(X_L0, g)

                def rest_of_msg(layer, g):
                    pool.wait_ge(msg_hi_ready, b * 2 * NG + (layer * NG + g + 1))
                    pool.tensor_sub(msg_lo[:, g * G:(g + 1) * G, :].rearrange("p t d -> p (t d)"), msg[:, g % 2, :],
                                    msg_hi[:, g * G:(g + 1) * G, :].rearrange("p t d -> p (t d)").bitcast(fp32))\
                        .then_inc(msg_ready, 1)

                def rest_of_adj(layer, n):
                    pool.wait_ge(hi_ready, b * 2 * TILES + (layer * TILES + n + 1))
                    free = lo_free(b, layer, n)
                    if free is not None:
                        pool.wait_ge(tile_used, free)
                    pool.tensor_sub(adj_lo[:, n % LO_SLOTS, :, LO_CUT:GN], piece(n)[:, :, LO_CUT:GN],
                                    adj_hi[:, n % HI_SLOTS, :, LO_CUT:GN].bitcast(fp32)).then_inc(lo_pool_ready, 1)

                mask_b = mask[:, b, :] if isinstance(b, int) else \
                    mask[:, bass.ds(b, 1), :].rearrange("p a t -> p (a t)")

                def grp(a, g):
                    return a[:, g * G:(g + 1) * G]

                for n in range(2):
                    rest_of_adj(0, n)
                for g in range(2):
                    rest_of_msg(0, g)
                for layer in range(2):
                    for n in range(0 if layer else 2, TILES):
                        rest_of_adj(layer, n)
                        if layer == 0 and n == HI_SLOTS:
                            rest_of_msg(0, 2)
                        for m, g in behind(later(MSG_AFTER, 5), layer, n):
                            rest_of_msg(m, g)
                        g = n - MASK_AFTER
                        if layer == 1 and 0 <= g < NG:
                            pool.wait_ge(msg_ready, b * 2 * NG + 2 * NG)
                            pool.tensor_mul(grp(x1m, g), boutb[:, :].unsqueeze(1).to_broadcast([P, G, C]),
                                            grp(mask_b, g).unsqueeze(2).to_broadcast([P, G, C]))\
                                .then_inc(bout_masked, 1)
                        g = n - X1M_AFTER
                        if layer == 1 and 0 <= g < NG:
                            pool.wait_ge(bout_masked, b * NG + (g + 1))
                            pool.tensor_add(grp(x1m, g), grp(x1m, g), grp(xa, g)).then_inc(x1m_ready, 1)
                        if layer == 1 and n in POWER_AFTER:
                            norm(X_L1, POWER_AFTER.index(n))
                for g in range(2, NG):
                    norm(X_L1, g)
                    add_bias(g - 2)
                for g in range(2, NG):
                    add_bias(g)
                pool.wait_ge(rowsum_ready, b + 1)
                power(dinv[:, :], tiny[:, 1, :], T, dinv_ready)

                def add_eye(g):
                    pool.wait_ge(acc_done, b * ACC_ALL + (ACC_L2 + g + 1))
                    for k in range(g * G, (g + 1) * G):
                        block_kk = adjT_flat[:, k * (N + P):k * (N + P) + P]
                        last = pool.tensor_add(block_kk, block_kk, ident[:, :])
                    last.then_inc(eye_added, 1)

                add_eye(0)
                add_eye(1)
                for g in range(NG):
                    norm(X_L2, g)
                    if g == 0:
                        pool.wait_ge(dinv_set, b + 1)
                    pool.wait_ge(x_ready, b * X_ALL + (X_L2 + g + 1))
                    pool.tensor_mul(ys[:, g * G:(g + 1) * G, :], xb[:, g * G:(g + 1) * G, :],
                                    dinv[:, g * G:(g + 1) * G].unsqueeze(2).to_broadcast([P, G, C]))\
                        .then_inc(ys_ready, 1)
                add_eye(2)
                add_eye(3)
                for g in range(NG):
                    norm(X_L3, g)

            pool.wait_ge(u_split, 1)
            with pool.Fori(0, B - 1) as b:
                batch(b, False)
            batch(B - 1, True)


CONSTS = 8 + 3 + 4 + 2 + 1


_INS = ['x', 'adj', 'nodemask', 'L0_gnn_U', 'L0_gnn_w_scale', 'L1_gnn_W0', 'L1_gnn_b0', 'L1_gnn_W1', 'L1_gnn_b1',
        'L1_gnn_W2', 'L1_gnn_b2', 'L1_gnn_Wout', 'L1_gnn_bout', 'L2_gnn_W_neighbors', 'L2_gnn_W_self',
        'L2_gnn_bias', 'L3_gnn_kernel']


def kernel(**inputs):
    import concourse.bacc as _bacc
    from concourse.bass_utils import run_bass_kernel_spmd as _run

    nc = _bacc.Bacc("TRN2", target_bir_lowering=False, num_devices=1)
    arrays, args = {}, []
    for name in _INS:
        a = np.ascontiguousarray(inputs[name])
        if a.ndim == 0:
            a = a.reshape(1)
        if name == 'nodemask':
            a = np.ascontiguousarray(a.reshape(a.shape[0], -1, 128).transpose(2, 0, 1))
        arrays[f"in_{name}"] = a
        args.append(nc.dram_tensor(f"in_{name}", a.shape, mybir.dt.from_np(a.dtype), kind="ExternalInput").ap())
    shape = inputs['x'].shape
    args.append(nc.dram_tensor("out_x", shape, mybir.dt.float32, kind="ExternalOutput").ap())
    adjacency_stack_kernel(nc, *args)
    r = _run(nc, [arrays], core_ids=[0])
    return r.results[0]["out_x"]
```
